# Optimizing a Trainium2 kernel written in Bass

```python
import numpy as np
import jax
import jax.numpy as jnp

def _softmax(x, axis=-1):
    return jax.nn.softmax(x, axis=axis)

def _gelu(x):
    return jax.nn.gelu(x, approximate=True)

def _silu(x):
    return jax.nn.silu(x)

def _sigmoid(x):
    return jax.nn.sigmoid(x)

def _layernorm(x, axis=-1, eps=1e-05):
    m = jnp.mean(x, axis=axis, keepdims=True)
    v = jnp.var(x, axis=axis, keepdims=True)
    return (x - m) / jnp.sqrt(v + eps)

def _scatter_add(tgt, idx, src, axis=0):
    return tgt.at[idx].add(src)

def _segment_sum(src, seg, n):
    return jax.ops.segment_sum(src, seg, n)
kernel_name = 'mk_seq_preln_d2_jaxref_r4_89e0f9'

def setup_inputs(seed: int=0):
    np.random.seed(seed)
    _w = jnp.asarray

    def _L0_attn_setup():
        import jax, jax.numpy as jnp
        import numpy as np
        BATCH, SEQ, HID, INTER, NSTATE, DTRANK, KCONV = (1, 256, 512, 1024, 16, 128, 4)
        EPS = 1e-06

        def _rms(x):
            x32 = x.astype(jnp.float32)
            return (x32 * jax.lax.rsqrt(jnp.mean(x32 * x32, axis=-1, keepdims=True) + EPS)).astype(x.dtype)
        key = jax.random.key(seed)
        ks = jax.random.split(key, 8)
        x = jax.random.normal(ks[0], (BATCH, SEQ, HID), jnp.float32)
        in_proj_w = jax.random.normal(ks[1], (HID, 2 * INTER), jnp.float32) * 0.02
        conv_w = jax.random.normal(ks[2], (INTER, 1, KCONV), jnp.float32) * 0.2
        conv_b = jnp.zeros((INTER,), jnp.float32)
        x_proj_w = jax.random.normal(ks[3], (INTER, DTRANK + 2 * NSTATE), jnp.float32) * 0.02
        dt_proj_w = jax.random.normal(ks[4], (DTRANK, INTER), jnp.float32) * DTRANK ** (-0.5)
        dt_proj_b = jax.random.normal(ks[5], (INTER,), jnp.float32) * 0.1
        out_proj_w = jax.random.normal(ks[6], (INTER, HID), jnp.float32) * 0.02
        A_log = jnp.log(jnp.broadcast_to(jnp.arange(1, NSTATE + 1, dtype=jnp.float32), (INTER, NSTATE)))
        D_param = jnp.ones((INTER,), jnp.float32)
        return {'x': x, 'in_proj_w': in_proj_w, 'conv_w': conv_w, 'conv_b': conv_b, 'x_proj_w': x_proj_w, 'dt_proj_w': dt_proj_w, 'dt_proj_b': dt_proj_b, 'out_proj_w': out_proj_w, 'A_log': A_log, 'D_param': D_param}
    _L0_attn_in = _L0_attn_setup()

    def _L0_ffn_setup():
        import math
        import jax, jax.numpy as jnp
        import numpy as np
        DIM = 512
        RANK = 8
        B, T = (4, 1024)

        def _orthogonal(key, n):
            a = jax.random.normal(key, (n, n), dtype=jnp.float32)
            q, r = jnp.linalg.qr(a)
            q = q * jnp.sign(jnp.diagonal(r))[None, :]
            return q
        key = jax.random.key(seed)
        kx, kf = jax.random.split(key)
        x = jax.random.normal(kx, (B, T, DIM), dtype=jnp.float32)
        fkeys = jax.random.split(kf, RANK)
        factors = jnp.stack([_orthogonal(fkeys[r], DIM) * (r + 1) ** (-0.5) for r in range(RANK)])
        bias = jnp.zeros((DIM,), dtype=jnp.float32)
        return {'x': x, 'factors': factors, 'bias': bias}
    _L0_ffn_in = _L0_ffn_setup()

    def _L1_attn_setup():
        import math
        import jax, jax.numpy as jnp
        import numpy as np
        EMBED_DIM = 512
        NUM_HEADS = 16
        HEAD_DIM = EMBED_DIM // NUM_HEADS
        CHUNK = 128
        RMS_EPS = 1e-05

        def _build_slopes(n):

            def pow2(n):
                start = 2.0 ** (-2.0 ** (-(math.log2(n) - 3)))
                return [start * start ** i for i in range(n)]
            if math.log2(n).is_integer():
                s = pow2(n)
            else:
                closest = 2 ** math.floor(math.log2(n))
                s = pow2(closest) + pow2(2 * closest)[0::2][:n - closest]
            return jnp.asarray(s, dtype=jnp.float32)

        def _rotary(x_BTHD, offset=0):
            T, D = (x_BTHD.shape[1], x_BTHD.shape[-1])
            freq = (1.0 / 1024.0) ** jnp.linspace(0.0, 1.0, D // 4, dtype=jnp.float32)
            freq = jnp.concatenate([freq, jnp.zeros(D // 4, dtype=jnp.float32)])
            t = jnp.arange(offset, offset + T, dtype=jnp.float32)
            theta = t[:, None] * freq[None, :]
            cos = jnp.cos(theta)[None, :, None, :]
            sin = jnp.sin(theta)[None, :, None, :]
            x1, x2 = jnp.split(x_BTHD.astype(jnp.float32), 2, axis=-1)
            y1 = x1 * cos + x2 * sin
            y2 = -x1 * sin + x2 * cos
            return jnp.concatenate([y1, y2], axis=-1).astype(x_BTHD.dtype)

        def _lightning_attn(q, k, v, slopes):
            B, H, T, D = q.shape
            C = CHUNK
            NC = T // C
            r = jnp.exp(-slopes)
            i = jnp.arange(C, dtype=jnp.float32)
            q_decay = r[:, None] ** (i[None, :] + 1.0)
            k_decay = r[:, None] ** (C - 1.0 - i[None, :])
            diff = i[:, None] - i[None, :]
            mask = diff >= 0
            dmask = jnp.where(mask[None], r[:, None, None] ** jnp.where(mask, diff, 0.0)[None], 0.0)
            r_C = r ** float(C)

            def reshape_chunks(x):
                return x.reshape(B, H, NC, C, D).transpose(2, 0, 1, 3, 4)
            qc, kc, vc = (reshape_chunks(q), reshape_chunks(k), reshape_chunks(v))

            def step(kv, qkv):
                qi, ki, vi = qkv
                inter = jnp.einsum('bhcd,bhde->bhce', qi * q_decay[None, :, :, None], kv)
                scores = jnp.einsum('bhcd,bhsd->bhcs', qi, ki) * dmask[None]
                intra = jnp.einsum('bhcs,bhse->bhce', scores, vi)
                kv_new = r_C[None, :, None, None] * kv + jnp.einsum('bhcd,bhce->bhde', ki * k_decay[None, :, :, None], vi)
                return (kv_new, inter + intra)
            kv0 = jnp.zeros((B, H, D, D), dtype=q.dtype)
            _, out = jax.lax.scan(step, kv0, (qc, kc, vc))
            return out.transpose(1, 2, 0, 3, 4).reshape(B, H, T, D)

        def _rms_norm(x, w):
            var = jnp.mean(jnp.square(x), axis=-1, keepdims=True)
            return x * jax.lax.rsqrt(var + RMS_EPS) * w
        key = jax.random.key(seed)
        ks = jax.random.split(key, 6)
        sc = 1.0 / math.sqrt(EMBED_DIM)
        return {'x': jax.random.normal(ks[0], (4, 1024, EMBED_DIM), dtype=jnp.float32), 'Wq': jax.random.normal(ks[1], (EMBED_DIM, EMBED_DIM), dtype=jnp.float32) * sc, 'Wk': jax.random.normal(ks[2], (EMBED_DIM, EMBED_DIM), dtype=jnp.float32) * sc, 'Wv': jax.random.normal(ks[3], (EMBED_DIM, EMBED_DIM), dtype=jnp.float32) * sc, 'Wo': jax.random.normal(ks[4], (EMBED_DIM, EMBED_DIM), dtype=jnp.float32) * sc, 'rms_w': jnp.ones((EMBED_DIM,), dtype=jnp.float32)}
    _L1_attn_in = _L1_attn_setup()

    def _L1_ffn_setup():
        import jax, jax.numpy as jnp
        import numpy as np
        D_MODEL = 512
        NUM_TILES = 64
        D_SLICE = D_MODEL // NUM_TILES
        TILES_PER_CLUSTER = 8
        NUM_CLUSTERS = NUM_TILES // TILES_PER_CLUSTER
        GRID = 16
        LN_EPS = 1e-05
        DIMS = (np.arange(NUM_TILES)[:, None] * D_SLICE + np.arange(D_SLICE)[None, :]) % D_MODEL
        DIMS = jnp.asarray(DIMS, dtype=jnp.int32)

        def _forward(x, ln_gamma, ln_beta, spline_bases, spline_slopes, output_scale):
            B, S, D = x.shape
            N = B * S
            mu = jnp.mean(x, axis=-1, keepdims=True)
            var = jnp.mean(jnp.square(x - mu), axis=-1, keepdims=True)
            xn = (x - mu) * jax.lax.rsqrt(var + LN_EPS) * ln_gamma + ln_beta
            xf = xn.reshape(N, D)
            slope_sign = jnp.sign(jnp.mean(spline_slopes, axis=-1))
            tile_sigs = jnp.zeros((NUM_TILES, D), dtype=x.dtype)
            tile_sigs = tile_sigs.at[jnp.arange(NUM_TILES)[:, None], DIMS].set(slope_sign)
            cluster_sigs = jnp.sign(tile_sigs.reshape(NUM_CLUSTERS, TILES_PER_CLUSTER, D).mean(axis=1))
            cluster_assign = jnp.arange(NUM_TILES, dtype=jnp.int32) // TILES_PER_CLUSTER
            input_sigs = jnp.sign(xf)
            cluster_scores = input_sigs @ cluster_sigs.T
            best_cluster = jnp.argmax(cluster_scores, axis=-1)
            tile_scores = input_sigs @ tile_sigs.T
            in_cluster = cluster_assign[None, :] == best_cluster[:, None]
            tile_idx = jnp.argmax(jnp.where(in_cluster, tile_scores, -jnp.inf), axis=-1)
            tok_dims = DIMS[tile_idx]
            x_slice = jnp.take_along_axis(xf, tok_dims, axis=1)
            tok_min = x_slice.min(axis=1)
            tok_max = x_slice.max(axis=1)
            onehot = tile_idx[None, :] == jnp.arange(NUM_TILES)[:, None]
            tile_min = jnp.where(onehot, tok_min[None, :], jnp.inf).min(axis=1)
            tile_max = jnp.where(onehot, tok_max[None, :], -jnp.inf).max(axis=1)
            mn = tile_min[tile_idx][:, None]
            mx = tile_max[tile_idx][:, None]
            u = jnp.clip((x_slice - mn) / (mx - mn + 1e-08), 0.0, 1.0 - 1e-06)
            gi = jnp.clip((u * GRID).astype(jnp.int32), 0, GRID - 1)
            j = jnp.arange(D_SLICE)[None, :]
            b = spline_bases[tile_idx[:, None], j, gi]
            s = spline_slopes[tile_idx[:, None], j, gi]
            x_local = (u - gi.astype(u.dtype) / GRID) * GRID
            delta = (b + s * x_local) * output_scale[tile_idx][:, None]
            out = jnp.zeros_like(xf).at[jnp.arange(N)[:, None], tok_dims].set(delta)
            return x + out.reshape(B, S, D)
        key = jax.random.key(seed)
        k1, k2, k3, k4, k5, k6 = jax.random.split(key, 6)
        x = jax.random.normal(k1, (4, 1024, D_MODEL), dtype=jnp.float32)
        ln_gamma = 1.0 + 0.1 * jax.random.normal(k2, (D_MODEL,), dtype=jnp.float32)
        ln_beta = 0.1 * jax.random.normal(k3, (D_MODEL,), dtype=jnp.float32)
        spline_bases = 0.1 * jax.random.normal(k4, (NUM_TILES, D_SLICE, GRID), dtype=jnp.float32)
        spline_slopes = 0.1 + 0.1 * jax.random.normal(k5, (NUM_TILES, D_SLICE, GRID), dtype=jnp.float32)
        output_scale = 1.0 + 0.1 * jax.random.normal(k6, (NUM_TILES,), dtype=jnp.float32)
        return {'x': x, 'ln_gamma': ln_gamma, 'ln_beta': ln_beta, 'spline_bases': spline_bases, 'spline_slopes': spline_slopes, 'output_scale': output_scale}
    _L1_ffn_in = _L1_ffn_setup()
    _d = {'L0_attn_x': _L0_attn_in['x'], 'L0_attn_in_proj_w': _L0_attn_in['in_proj_w'], 'L0_attn_conv_w': _L0_attn_in['conv_w'], 'L0_attn_conv_b': _L0_attn_in['conv_b'], 'L0_attn_x_proj_w': _L0_attn_in['x_proj_w'], 'L0_attn_dt_proj_w': _L0_attn_in['dt_proj_w'], 'L0_attn_dt_proj_b': _L0_attn_in['dt_proj_b'], 'L0_attn_out_proj_w': _L0_attn_in['out_proj_w'], 'L0_attn_A_log': _L0_attn_in['A_log'], 'L0_attn_D_param': _L0_attn_in['D_param'], 'L0_ffn_factors': _L0_ffn_in['factors'], 'L0_ffn_bias': _L0_ffn_in['bias'], 'L1_attn_Wq': _L1_attn_in['Wq'], 'L1_attn_Wk': _L1_attn_in['Wk'], 'L1_attn_Wv': _L1_attn_in['Wv'], 'L1_attn_Wo': _L1_attn_in['Wo'], 'L1_attn_rms_w': _L1_attn_in['rms_w'], 'L1_ffn_ln_gamma': _L1_ffn_in['ln_gamma'], 'L1_ffn_ln_beta': _L1_ffn_in['ln_beta'], 'L1_ffn_spline_bases': _L1_ffn_in['spline_bases'], 'L1_ffn_spline_slopes': _L1_ffn_in['spline_slopes'], 'L1_ffn_output_scale': _L1_ffn_in['output_scale']}
    _x0 = _d['L0_attn_x']
    _d['L0_attn_x'] = jax.random.normal(jax.random.fold_in(jax.random.key(seed), 1), (2, 4096, 512), dtype=_x0.dtype)
    del _x0
    return _d

def reference(L0_attn_x, L0_attn_in_proj_w, L0_attn_conv_w, L0_attn_conv_b, L0_attn_x_proj_w, L0_attn_dt_proj_w, L0_attn_dt_proj_b, L0_attn_out_proj_w, L0_attn_A_log, L0_attn_D_param, L0_ffn_factors, L0_ffn_bias, L1_attn_Wq, L1_attn_Wk, L1_attn_Wv, L1_attn_Wo, L1_attn_rms_w, L1_ffn_ln_gamma, L1_ffn_ln_beta, L1_ffn_spline_bases, L1_ffn_spline_slopes, L1_ffn_output_scale):

    def _L0_attn_ref(x, in_proj_w, conv_w, conv_b, x_proj_w, dt_proj_w, dt_proj_b, out_proj_w, A_log, D_param):
        import jax, jax.numpy as jnp
        import numpy as np
        BATCH, SEQ, HID, INTER, NSTATE, DTRANK, KCONV = (1, 256, 512, 1024, 16, 128, 4)
        EPS = 1e-06

        def _rms(x):
            x32 = x.astype(jnp.float32)
            return (x32 * jax.lax.rsqrt(jnp.mean(x32 * x32, axis=-1, keepdims=True) + EPS)).astype(x.dtype)
        Bsz, L, _ = x.shape
        proj = x @ in_proj_w
        hidden, gate = jnp.split(proj, 2, axis=-1)
        h = jnp.swapaxes(hidden, 1, 2)
        h = jax.lax.conv_general_dilated(h, conv_w, window_strides=(1,), padding=((KCONV - 1, KCONV - 1),), feature_group_count=INTER)[..., :L]
        h = h + conv_b[None, :, None]
        hs = jnp.swapaxes(jax.nn.silu(h), 1, 2)
        ssm_p = hs @ x_proj_w
        dt, Bm, Cm = jnp.split(ssm_p, [DTRANK, DTRANK + NSTATE], axis=-1)
        Bm, Cm, dt = (_rms(Bm), _rms(Cm), _rms(dt))
        dt = jax.nn.softplus(dt @ dt_proj_w + dt_proj_b)
        A = -jnp.exp(A_log.astype(jnp.float32))
        dt32 = dt.astype(jnp.float32)
        u = hs.astype(jnp.float32)
        dA = jnp.exp(dt32[..., None] * A)
        dBu = (dt32 * u)[..., None] * Bm.astype(jnp.float32)[:, :, None, :]
        C32 = Cm.astype(jnp.float32)

        def step(s, inp):
            dA_t, dBu_t, C_t = inp
            s = dA_t * s + dBu_t
            y = jnp.einsum('bdn,bn->bd', s, C_t)
            return (s, y)
        s0 = jnp.zeros((Bsz, INTER, NSTATE), jnp.float32)
        _, ys = jax.lax.scan(step, s0, (jnp.swapaxes(dA, 0, 1), jnp.swapaxes(dBu, 0, 1), jnp.swapaxes(C32, 0, 1)))
        y = jnp.swapaxes(ys, 0, 1)
        y = y + u * D_param
        y = y * jax.nn.silu(gate)
        return y.astype(x.dtype) @ out_proj_w

    def _L0_ffn_ref(x, factors, bias):
        import math
        import jax, jax.numpy as jnp
        import numpy as np
        DIM = 512
        RANK = 8
        B, T = (4, 1024)

        def _orthogonal(key, n):
            a = jax.random.normal(key, (n, n), dtype=jnp.float32)
            q, r = jnp.linalg.qr(a)
            q = q * jnp.sign(jnp.diagonal(r))[None, :]
            return q
        rank = factors.shape[0]
        mixed = jnp.einsum('btd,rde->bte', x, factors)
        mixed = mixed / math.sqrt(rank) + bias
        return mixed

    def _L1_attn_ref(x, Wq, Wk, Wv, Wo, rms_w):
        import math
        import jax, jax.numpy as jnp
        import numpy as np
        EMBED_DIM = 512
        NUM_HEADS = 16
        HEAD_DIM = EMBED_DIM // NUM_HEADS
        CHUNK = 128
        RMS_EPS = 1e-05

        def _build_slopes(n):

            def pow2(n):
                start = 2.0 ** (-2.0 ** (-(math.log2(n) - 3)))
                return [start * start ** i for i in range(n)]
            if math.log2(n).is_integer():
                s = pow2(n)
            else:
                closest = 2 ** math.floor(math.log2(n))
                s = pow2(closest) + pow2(2 * closest)[0::2][:n - closest]
            return jnp.asarray(s, dtype=jnp.float32)

        def _rotary(x_BTHD, offset=0):
            T, D = (x_BTHD.shape[1], x_BTHD.shape[-1])
            freq = (1.0 / 1024.0) ** jnp.linspace(0.0, 1.0, D // 4, dtype=jnp.float32)
            freq = jnp.concatenate([freq, jnp.zeros(D // 4, dtype=jnp.float32)])
            t = jnp.arange(offset, offset + T, dtype=jnp.float32)
            theta = t[:, None] * freq[None, :]
            cos = jnp.cos(theta)[None, :, None, :]
            sin = jnp.sin(theta)[None, :, None, :]
            x1, x2 = jnp.split(x_BTHD.astype(jnp.float32), 2, axis=-1)
            y1 = x1 * cos + x2 * sin
            y2 = -x1 * sin + x2 * cos
            return jnp.concatenate([y1, y2], axis=-1).astype(x_BTHD.dtype)

        def _lightning_attn(q, k, v, slopes):
            B, H, T, D = q.shape
            C = CHUNK
            NC = T // C
            r = jnp.exp(-slopes)
            i = jnp.arange(C, dtype=jnp.float32)
            q_decay = r[:, None] ** (i[None, :] + 1.0)
            k_decay = r[:, None] ** (C - 1.0 - i[None, :])
            diff = i[:, None] - i[None, :]
            mask = diff >= 0
            dmask = jnp.where(mask[None], r[:, None, None] ** jnp.where(mask, diff, 0.0)[None], 0.0)
            r_C = r ** float(C)

            def reshape_chunks(x):
                return x.reshape(B, H, NC, C, D).transpose(2, 0, 1, 3, 4)
            qc, kc, vc = (reshape_chunks(q), reshape_chunks(k), reshape_chunks(v))

            def step(kv, qkv):
                qi, ki, vi = qkv
                inter = jnp.einsum('bhcd,bhde->bhce', qi * q_decay[None, :, :, None], kv)
                scores = jnp.einsum('bhcd,bhsd->bhcs', qi, ki) * dmask[None]
                intra = jnp.einsum('bhcs,bhse->bhce', scores, vi)
                kv_new = r_C[None, :, None, None] * kv + jnp.einsum('bhcd,bhce->bhde', ki * k_decay[None, :, :, None], vi)
                return (kv_new, inter + intra)
            kv0 = jnp.zeros((B, H, D, D), dtype=q.dtype)
            _, out = jax.lax.scan(step, kv0, (qc, kc, vc))
            return out.transpose(1, 2, 0, 3, 4).reshape(B, H, T, D)

        def _rms_norm(x, w):
            var = jnp.mean(jnp.square(x), axis=-1, keepdims=True)
            return x * jax.lax.rsqrt(var + RMS_EPS) * w
        B, T, E = x.shape
        H, D = (NUM_HEADS, HEAD_DIM)
        q = (x @ Wq).reshape(B, T, H, D)
        k = (x @ Wk).reshape(B, T, H, D)
        v = (x @ Wv).reshape(B, T, H, D)
        q = _rotary(q)
        k = _rotary(k)
        q, k, v = (t.transpose(0, 2, 1, 3) for t in (q, k, v))
        slopes = _build_slopes(H)
        attn = _lightning_attn(q, k, v, slopes)
        attn = attn.transpose(0, 2, 1, 3).reshape(B, T, E)
        attn = _rms_norm(attn, rms_w)
        return attn @ Wo

    def _L1_ffn_ref(x, ln_gamma, ln_beta, spline_bases, spline_slopes, output_scale):
        import jax, jax.numpy as jnp
        import numpy as np
        D_MODEL = 512
        NUM_TILES = 64
        D_SLICE = D_MODEL // NUM_TILES
        TILES_PER_CLUSTER = 8
        NUM_CLUSTERS = NUM_TILES // TILES_PER_CLUSTER
        GRID = 16
        LN_EPS = 1e-05
        DIMS = (np.arange(NUM_TILES)[:, None] * D_SLICE + np.arange(D_SLICE)[None, :]) % D_MODEL
        DIMS = jnp.asarray(DIMS, dtype=jnp.int32)

        def _forward(x, ln_gamma, ln_beta, spline_bases, spline_slopes, output_scale):
            B, S, D = x.shape
            N = B * S
            mu = jnp.mean(x, axis=-1, keepdims=True)
            var = jnp.mean(jnp.square(x - mu), axis=-1, keepdims=True)
            xn = (x - mu) * jax.lax.rsqrt(var + LN_EPS) * ln_gamma + ln_beta
            xf = xn.reshape(N, D)
            slope_sign = jnp.sign(jnp.mean(spline_slopes, axis=-1))
            tile_sigs = jnp.zeros((NUM_TILES, D), dtype=x.dtype)
            tile_sigs = tile_sigs.at[jnp.arange(NUM_TILES)[:, None], DIMS].set(slope_sign)
            cluster_sigs = jnp.sign(tile_sigs.reshape(NUM_CLUSTERS, TILES_PER_CLUSTER, D).mean(axis=1))
            cluster_assign = jnp.arange(NUM_TILES, dtype=jnp.int32) // TILES_PER_CLUSTER
            input_sigs = jnp.sign(xf)
            cluster_scores = input_sigs @ cluster_sigs.T
            best_cluster = jnp.argmax(cluster_scores, axis=-1)
            tile_scores = input_sigs @ tile_sigs.T
            in_cluster = cluster_assign[None, :] == best_cluster[:, None]
            tile_idx = jnp.argmax(jnp.where(in_cluster, tile_scores, -jnp.inf), axis=-1)
            tok_dims = DIMS[tile_idx]
            x_slice = jnp.take_along_axis(xf, tok_dims, axis=1)
            tok_min = x_slice.min(axis=1)
            tok_max = x_slice.max(axis=1)
            onehot = tile_idx[None, :] == jnp.arange(NUM_TILES)[:, None]
            tile_min = jnp.where(onehot, tok_min[None, :], jnp.inf).min(axis=1)
            tile_max = jnp.where(onehot, tok_max[None, :], -jnp.inf).max(axis=1)
            mn = tile_min[tile_idx][:, None]
            mx = tile_max[tile_idx][:, None]
            u = jnp.clip((x_slice - mn) / (mx - mn + 1e-08), 0.0, 1.0 - 1e-06)
            gi = jnp.clip((u * GRID).astype(jnp.int32), 0, GRID - 1)
            j = jnp.arange(D_SLICE)[None, :]
            b = spline_bases[tile_idx[:, None], j, gi]
            s = spline_slopes[tile_idx[:, None], j, gi]
            x_local = (u - gi.astype(u.dtype) / GRID) * GRID
            delta = (b + s * x_local) * output_scale[tile_idx][:, None]
            out = jnp.zeros_like(xf).at[jnp.arange(N)[:, None], tok_dims].set(delta)
            return x + out.reshape(B, S, D)
        return _forward(x, ln_gamma, ln_beta, spline_bases, spline_slopes, output_scale)
    x = L0_attn_x
    x = x + _L0_attn_ref(_layernorm(x, axis=-1), L0_attn_in_proj_w, L0_attn_conv_w, L0_attn_conv_b, L0_attn_x_proj_w, L0_attn_dt_proj_w, L0_attn_dt_proj_b, L0_attn_out_proj_w, L0_attn_A_log, L0_attn_D_param)
    x = x + _L0_ffn_ref(_layernorm(x, axis=-1), L0_ffn_factors, L0_ffn_bias)
    x = x + _L1_attn_ref(_layernorm(x, axis=-1), L1_attn_Wq, L1_attn_Wk, L1_attn_Wv, L1_attn_Wo, L1_attn_rms_w)
    x = x + _L1_ffn_ref(_layernorm(x, axis=-1), L1_ffn_ln_gamma, L1_ffn_ln_beta, L1_ffn_spline_bases, L1_ffn_spline_slopes, L1_ffn_output_scale)
    return x

_drawn_inputs = setup_inputs


def setup_inputs(seed=0):
    import zlib

    import numpy as np

    out = dict(_drawn_inputs(seed))
    spreads = {'L0_attn_conv_b': (0.0, 0.1),
     'L0_attn_D_param': (1.0, 0.6),
     'L0_ffn_bias': (0.0, 0.1),
     'L1_attn_rms_w': (1.0, 0.2)}
    factors = {'L0_attn_dt_proj_b': 8.0,
     'L0_attn_A_log': 3.811,
     'L1_ffn_ln_gamma': 8.0,
     'L1_ffn_ln_beta': 8.0,
     'L1_ffn_spline_bases': 8.0,
     'L1_ffn_spline_slopes': 8.0,
     'L1_ffn_output_scale': 8.0}
    for name, (base, spread) in spreads.items():
        noise = np.random.default_rng([zlib.crc32(name.encode()), seed]).standard_normal(out[name].shape)
        drawn = base * np.exp(spread * noise) if base else spread * noise
        out[name] = jnp.asarray(drawn.astype(out[name].dtype))
    for name, factor in factors.items():
        out[name] = (out[name] * factor).astype(out[name].dtype)
    return out
```

```python
import numpy as np
import concourse.bass as bass
from concourse import mybir
from contextlib import ExitStack

F32 = mybir.dt.float32
BF16 = mybir.dt.bfloat16
I32 = mybir.dt.int32
ALU = mybir.AluOpType
ACT = mybir.ActivationFunctionType
AX = mybir.AxisListType

P = 128
T = 512
NT = T // P
LN_EPS = 1e-5
SSM_EPS = 1e-6
EXP_LN_SET = "natural_log_exp_and_others"


def wait(eng, sem, value):
    if not isinstance(value, int) or value > 0:
        eng.wait_ge(sem, value)


class Ring:

    def __init__(self, order, full, taken):
        self.order, self.full, self.taken = order, full, taken
        self.at = {use: q for q, (use, _) in enumerate(order)}
        self.per = {e: sum(1 for _, x in order if x == e) for e in taken}

    def bank(self, use):
        return self.at[use] % 2

    def filled(self, use, period):
        return period * len(self.order) + self.at[use] + 1

    def emptied(self, use, period):
        q = self.at[use]
        e = self.order[q][1]
        return self.taken[e], period * self.per[e] + sum(1 for _, x in self.order[:q + 1] if x == e)

    def before(self, use, period):
        q = self.at[use] - 2
        if q >= 0:
            return self.emptied(self.order[q][0], period)
        sem, value = self.emptied(self.order[q + len(self.order)][0], period)
        return sem, value - self.per[self.order[q + len(self.order)][1]]


def mamba_block(nc, x, in_w, chan, xproj_w, dt_w, out_w, eye, x1):
    BATCH, SEQ, HID = x.shape
    INTER = in_w.shape[1] // 2
    NSTATE = (xproj_w.shape[1] - dt_w.shape[0]) // 2
    RANK = dt_w.shape[0]
    KB = HID // P
    G = INTER // P
    GH = G // 2
    U = 2 * NSTATE
    SP_ = RANK + 2 * NSTATE
    NI = SEQ // T
    NCH = BATCH * NI
    assert BATCH == 2 and RANK == P and GH == 4 and NT == 4
    x_v = x.rearrange("b (i j p) d -> b i p j d", j=NT, p=P)
    x1_v = x1.rearrange("b (i j p) d -> b i j p d", j=NT, p=P)

    ctx = ExitStack()
    with ctx:
        def sb(name, shape, dt=F32):
            return ctx.enter_context(nc.sbuf_tensor(name, shape, dt))

        def ps(name, shape):
            return ctx.enter_context(nc.psum_tensor(name, shape, F32))

        def sem(name):
            return ctx.enter_context(nc.semaphore(name))

        w_in = sb("w_in", [P, KB, 2 * INTER])
        w_xp = sb("w_xp", [P, G, SP_])
        w_dt = sb("w_dt", [P, INTER])
        w_out = sb("w_out", [P, G, HID])
        ch = sb("ch", [P, G, 7 + NSTATE])
        ident = sb("ident", [P, P])
        minus_half = sb("minus_half", [P, NT * 3])
        xt = sb("xt", [P, NT, HID])
        xnT = sb("xnT", [P, KB, T])
        hid = [sb(f"hid{i}", [P, T + 3]) for i in range(2)]
        hist = sb("hist", [P, BATCH, G, 3])
        u = [sb(f"u{i}", [P, G, T]) for i in range(2)]
        gate = sb("gate", [P, G, T])
        dt = [sb(f"dt{i}", [P, GH, T]) for i in range(2)]
        dtu = sb("dtu", [P, GH, T])
        dbu = [sb(f"dbu{i}", [P, GH, T]) for i in range(2)]
        s = [sb(f"s{i}", [P, GH, T]) for i in range(2)]
        Bb = [sb(f"Bb{i}", [P, T]) for i in range(2)]
        Cb = [sb(f"Cb{i}", [P, T]) for i in range(2)]
        state = sb("state", [P, BATCH, U, GH])
        res = [sb(f"res{i}", [P, HID]) for i in range(2)]
        ssm = sb("ssm", [P, NT, SP_])
        dtnT = sb("dtnT", [P, T])
        bcT = sb("bcT", [2 * NSTATE, T])
        st6 = sb("st6", [P, NT, 6])
        mv = sb("mv", [P, NT, 2])
        ve = sb("ve", [P, NT])
        rstd = sb("rstd", [P, NT])
        ssq = sb("ssq", [P, NT, 3])
        rssm = sb("rssm", [P, NT, 3])

        Y = [ps(f"Y{g}", [P, T]) for g in range(GH)]
        DA = [ps(f"DA{i}", [P, T]) for i in range(2)]
        PJ = [ps(f"PJ{i}", [P, T]) for i in range(2)]
        bc = [nc.dram_tensor(f"bc{i}", (2 * NSTATE, T), F32, kind="Internal").ap() for i in range(2)]

        w_loaded, x_loaded = sem("w_loaded"), sem("x_loaded")
        consts_ready = sem("consts_ready")
        stats_ready, rstd_ready, xn_ready = sem("stats_ready"), sem("rstd_ready"), sem("xn_ready")
        conv_done, u_ready, gate_ready = sem("conv_done"), sem("u_ready"), sem("gate_ready")
        sq_ready, ssq_ready, rssm_ready, ssm_ready = (
            sem("sq_ready"), sem("ssq_ready"), sem("rssm_ready"), sem("ssm_ready"))
        dt_min, dt_log, dt_ready, dtu_ready = sem("dt_min"), sem("dt_log"), sem("dt_ready"), sem("dtu_ready")
        bc_stored, sp_steps = sem("bc_stored"), sem("sp_steps")
        b_loaded = [sem(f"b_loaded{i}") for i in range(2)]
        c_loaded = [sem(f"c_loaded{i}") for i in range(2)]
        dbu_ready, da_ready, scan_done, state_saved = (
            sem("dbu_ready"), sem("da_ready"), sem("scan_done"), sem("state_saved"))
        z_ready, sum_done, y_taken, y_ready = sem("z_ready"), sem("sum_done"), sem("y_taken"), sem("y_ready")
        res_loaded = [sem(f"res_loaded{i}") for i in range(2)]
        x1_ready = sem("x1_ready")
        x1_stored = [sem(f"x1_stored{i}") for i in range(2)]

        def ring(order, tag):
            return Ring(order, sem(f"proj_full_{tag}"),
                        {"act": sem(f"proj_taken_act_{tag}"), "dve": sem(f"proj_taken_dve_{tag}")})

        def uses(name, n, e):
            return [((name, j), e) for j in range(n)]

        ahead = ring(uses("xT", KB, "act") + uses("hid", G, "act") + uses("xp", 2, "dve")
                     + uses("turn", 2, "act") + uses("dt0", GH, "act"), "ahead")
        steady = ring(uses("gate", G, "act") + uses("xT", KB, "act") + uses("out", 1, "dve")
                      + uses("dt1", 2, "act") + [(("out", 1), "dve")]
                      + [(("dt1", 2), "act"), (("dt1", 3), "act"), (("out", 2), "dve"), (("out", 3), "dve")]
                      + uses("hid", G, "act") + uses("xp", 2, "dve") + uses("turn", 2, "act")
                      + uses("dt0", GH, "act"), "steady")
        after = ring(uses("out", NT, "dve"), "after")

        BLOCKS = ([("gate", m, None) for m in range(G)]
                  + [("out", j, part) for j in range(NT) for part in range(2)]
                  + [("hid", m, None) for m in range(G)])

        def blocks(k):
            return BLOCKS[4 * k // 3:4 * (k + 1) // 3]

        UNIT_OF = {b: k for k in range(18) for b in blocks(k)}
        K_XT, K_DT1, K_XP, K_TURN, K_DT0 = 6, (8, 9), (20, 21), 24, (25, 26)

        block = ctx.enter_context(nc.Block())

        def periods(eng, body):
            for b in range(BATCH):
                body(0, b, b, True and b == 0, False)
            with eng.Fori(1, NI - 1) as i:
                for b in range(BATCH):
                    body(i, b, i * BATCH + b, False, False)
            for b in range(BATCH):
                body(NI - 1, b, (NI - 1) * BATCH + b, False, b == BATCH - 1)

        @block.sync
        def _(sp):
            def held(sem_, value):
                wait(sp, sem_, value)
                sp.sem_inc(sp_steps, 1)

            for m in range(KB):
                sp.dma_start(w_in[:, m, :], in_w[m * P:(m + 1) * P, :]).then_inc(w_loaded, 16)
            sp.dma_start(w_xp[:], xproj_w.rearrange("(g p) n -> p g n", p=P)).then_inc(w_loaded, 16)
            sp.dma_start(w_dt[:], dt_w).then_inc(w_loaded, 16)
            sp.dma_start(w_out[:], out_w.rearrange("(g p) n -> p g n", p=P)).then_inc(w_loaded, 16)

            def load_b(c, k, slot):
                held( dbu_ready, c * U + (k - 1))
                sp.dma_start(Bb[k % 2][:], bc[slot][k % NSTATE:k % NSTATE + 1, :].to_broadcast([P, T])
                             ).then_inc(b_loaded[k % 2], 16)

            def load_c(c, k, slot):
                held( z_ready, c * U + (k - 1))
                sp.dma_start(Cb[k % 2][:], bc[slot][NSTATE + k % NSTATE:NSTATE + k % NSTATE + 1, :]
                             .to_broadcast([P, T])).then_inc(c_loaded[k % 2], 16)

            def store_bc(ring_, period, c_next, slot):
                s_, v = ring_.emptied(("turn", 1), period)
                held( s_, v)
                sp.dma_start(bc[slot], bcT[:]).then_inc(bc_stored, 16)

            store_bc(ahead, 0, 0, 0)
            sp.wait_ge(bc_stored, 16)
            for k in range(2):
                load_b(0, k, 0)
                load_c(0, k, 0)

            def load_res(i_prev, b_prev, c_prev, j):
                held( x1_stored[j % 2], 16 * (c_prev * 2 + j // 2))
                sp.dma_start(res[j % 2][:], x_v[b_prev, i_prev, :, j, :]).then_inc(res_loaded[j % 2], 16)

            def store_x1(i_prev, b_prev, c_prev, j):
                held( x1_ready, c_prev * NT + j + 1)
                sp.dma_start(x1_v[b_prev, i_prev, j], res[j % 2][:]).then_inc(x1_stored[j % 2], 16)

            def body(i, b, c, first, last):
                i_prev, b_prev, c_prev = (i, 0, c - 1) if b else (i - 1, 1, c - 1)
                i_next, b_next = (i + 1, 0) if b else (i, 1)
                for k in range(U):
                    if k == 0 and not last:
                        held( dt_ready, c * 2 + 1)
                        sp.dma_start(xt[:], x_v[b_next, i_next]).then_inc(x_loaded, 16)
                    if not first:
                        if k in (1, 2):
                            load_res(i_prev, b_prev, c_prev, k - 1)
                        if k in (9, 11):
                            store_x1(i_prev, b_prev, c_prev, (k - 9) // 2)
                            load_res(i_prev, b_prev, c_prev, (k - 9) // 2 + 2)
                        if k in (12, 13):
                            store_x1(i_prev, b_prev, c_prev, k - 10)
                    if k == 26 and not last:
                        store_bc(steady, c, c + 1, 1 - b)
                    if k + 2 < U:
                        load_b(c, k + 2, b)
                        load_c(c, k + 2, b)
                    elif not last:
                        if k + 2 == U:
                            held( bc_stored, 16 * (c + 2))
                        held( dbu_ready, c * U + k + 1)
                        n = k + 2 - U
                        sp.dma_start(Bb[n % 2][:], bc[1 - b][n:n + 1, :].to_broadcast([P, T])
                                     ).then_inc(b_loaded[n % 2], 16)
                        held( z_ready, c * U + k + 1)
                        sp.dma_start(Cb[n % 2][:], bc[1 - b][NSTATE + n:NSTATE + n + 1, :]
                                     .to_broadcast([P, T])).then_inc(c_loaded[n % 2], 16)

            periods(sp, body)
            for j in range(NT):
                load_res(NI - 1, 1, NCH - 1, j)
                store_x1(NI - 1, 1, NCH - 1, j)
            for j in range(2):
                sp.wait_ge(x1_stored[j], 16 * 2 * NCH)

        @block.gpsimd
        def _(pool):
            nc.gpsimd.memset(minus_half[:], -0.5)
            nc.gpsimd.memset(state[:], 0.0)
            nc.gpsimd.memset(hist[:], 0.0)
            pool.drain().then_inc(consts_ready, 1)

            def ln_power(c_next):
                wait(pool, stats_ready, c_next + 1)
                nc.gpsimd.tensor_tensor(rstd[:], ve[:], minus_half[:, 0:NT], ALU.pow).then_inc(rstd_ready, 1)

            def ssm_power(c_next):
                wait(pool, ssq_ready, c_next + 1)
                nc.gpsimd.tensor_tensor(rssm[:].rearrange("p j n -> p (j n)"), ssq[:].rearrange("p j n -> p (j n)"),
                                        minus_half[:], ALU.pow).then_inc(rssm_ready, 1)

            ln_power(0)
            ssm_power(0)

            def body(i, b, c, first, last):
                for k in range(U):
                    h = k // NSTATE
                    if k == 4 and not last:
                        ln_power(c + 1)
                    if k == 24 and not last:
                        ssm_power(c + 1)
                    if k % NSTATE == 0:
                        wait(pool, dt_ready, 2 * c + h + 1)
                        wait(pool, dbu_ready, c * U + k)
                        nc.gpsimd.tensor_tensor(dtu[:], dt[h][:], u[b][:, GH * h:GH * h + GH, :], ALU.mult
                                                ).then_inc(dtu_ready, 1)
                        wait(pool, dtu_ready, 2 * c + h + 1)
                    wait(pool, b_loaded[k % 2], 16 * (c * (U // 2) + k // 2 + 1))
                    wait(pool, scan_done, GH * (c * U + k - 1))
                    nc.gpsimd.tensor_tensor(dbu[k % 2][:], dtu[:], Bb[k % 2][:].unsqueeze(1).to_broadcast([P, GH, T]),
                                            ALU.mult).then_inc(dbu_ready, 1)

            periods(pool, body)

        @block.scalar
        def _(act):
            act.dma_start(ch[:], chan).then_inc(w_loaded, 16)
            act.dma_start(ident[:], eye).then_inc(w_loaded, 16)
            act.dma_start(xt[:], x_v[0, 0]).then_inc(x_loaded, 16)
            act.wait_ge(w_loaded, 16 * (KB + 5))
            nc.scalar.preload_act_table_set(EXP_LN_SET)
            nc.scalar.activation(ch[:, :, 7:], ch[:, :, 7:], ACT.Exp)
            act.drain()
            nc.scalar.mul(ch[:, :, 7:], ch[:, :, 7:], -1.0)
            act.drain().then_inc(consts_ready, 1)

            def take(ring_, use, period, out, part=P):
                act.wait_ge(ring_.full, ring_.filled(use, period))
                nc.scalar.copy(out, PJ[ring_.bank(use)][0:part, :]).then_inc(ring_.taken["act"], 1)

            def take_hid(ring_, m, period, c_next):
                wait(act, conv_done, c_next * G + m - 1)
                take(ring_, ("hid", m), period, hid[m % 2][:, 3:T + 3])

            def silu_u(c_next, slot):
                act.wait_ge(conv_done, (c_next + 1) * G)
                nc.scalar.activation(u[slot][:], u[slot][:], ACT.Silu).then_inc(u_ready, 1)

            def square(ring_, n, period):
                act.wait_ge(ring_.full, ring_.filled(("xp", n), period))
                nc.scalar.activation(ssm[:, 2 * n:2 * n + 2, :],
                                     PJ[ring_.bank(("xp", n))][:, 0:2 * SP_].rearrange("p (j n) -> p j n", j=2),
                                     ACT.Square).then_inc(sq_ready, 1)

            def turned(ring_, period, c_next):
                take(ring_, ("turn", 0), period, dtnT[:])
                wait(act, bc_stored, 16 * c_next)
                take(ring_, ("turn", 1), period, bcT[:], 2 * NSTATE)

            def dt_bias(ring_, h, g, period):
                use = (f"dt{h}", g)
                act.wait_ge(ring_.full, ring_.filled(use, period))
                nc.scalar.activation(dt[h][:, g, :], PJ[ring_.bank(use)][:], ACT.Identity,
                                     bias=ch[:, GH * h + g, 6:7]).then_inc(ring_.taken["act"], 1)

            def dt_exp_log(n):
                act.wait_ge(dt_min, n + 1)
                nc.scalar.activation(xt[:], xt[:], ACT.Exp)
                act.drain()
                nc.scalar.activation(xt[:], xt[:], ACT.Ln, bias=1.0).then_inc(dt_log, 1)

            for kb in range(KB):
                take(ahead, ("xT", kb), 0, xnT[:, kb, :])
            for m in range(G):
                take_hid(ahead, m, 0, 0)
            silu_u(0, 0)
            for n in range(2):
                square(ahead, n, 0)
            nc.scalar.preload_act_table_set(EXP_LN_SET)
            turned(ahead, 0, 0)
            for g in range(GH):
                dt_bias(ahead, 0, g, 0)
            dt_exp_log(0)

            def body(i, b, c, first, last):
                nc.scalar.preload_act_table_set(EXP_LN_SET)

                def piece(k):
                    for kind, m, _ in (blocks(k) if 0 <= k < 18 else ()):
                        if kind == "gate":
                            if m == 0:
                                wait(act, y_ready, 2 * c)
                            take(steady, ("gate", m), c, gate[:, m, :])
                        if kind == "hid" and not last:
                            take_hid(steady, m, c, c + 1)
                    if k == K_XT:
                        if last:
                            act.drain().then_inc(steady.taken["act"], KB)
                        else:
                            for kb in range(KB):
                                take(steady, ("xT", kb), c, xnT[:, kb, :])
                    if k in K_DT1:
                        for g in ((0, 1) if k == K_DT1[0] else (2, 3)):
                            dt_bias(steady, 1, g, c)
                    if k == 10:
                        dt_exp_log(2 * c + 1)
                    if k == 18:
                        nc.scalar.activation(gate[:], gate[:], ACT.Silu).then_inc(gate_ready, 1)
                        if not last:
                            silu_u(c + 1, 1 - b)
                        nc.scalar.preload_act_table_set(EXP_LN_SET)
                    if last:
                        return
                    if k in K_XP:
                        square(steady, k - K_XP[0], c)
                    if k == K_TURN:
                        turned(steady, c, c + 1)
                    if k in K_DT0:
                        for g in ((0, 1) if k == K_DT0[0] else (2, 3)):
                            dt_bias(steady, 0, g, c)
                    if k == 27:
                        dt_exp_log(2 * c + 2)

                for k in range(U):
                    h, n = k // NSTATE, k % NSTATE
                    for g in range(GH):
                        if n == 0 and g == 0:
                            wait(act, dt_ready, 2 * c + h + 1)
                        wait(act, scan_done, GH * (c * U + k) + g - 1)
                        nc.scalar.activation(DA[g % 2][:], dt[h][:, g, :], ACT.Exp,
                                             scale=ch[:, GH * h + g, 7 + n:8 + n]).then_inc(da_ready, 1)
                        if g == 1:
                            piece(k - 1)

            periods(act, body)

        @block.vector
        def _(dve):
            def ln_stats(c_next):
                wait(dve, x_loaded, 16 * (c_next + 1))
                for j in range(NT):
                    nc.vector.bn_stats(st6[:, j, :], xt[:, j, :])
                dve.drain()
                for j in range(NT):
                    nc.vector.bn_aggr(mv[:, j, :], st6[:, j, :])
                dve.drain()
                nc.vector.tensor_scalar(ve[:], mv[:, :, 1], 1.0, LN_EPS, ALU.mult, ALU.add).then_inc(stats_ready, 1)

            def ln_apply(c_next):
                wait(dve, rstd_ready, c_next + 1)
                for j in range(NT):
                    last_ = nc.vector.tensor_scalar(xt[:, j, :], xt[:, j, :], mv[:, j, 0:1], rstd[:, j:j + 1],
                                                    ALU.subtract, ALU.mult)
                last_.then_inc(xn_ready, 1)

            def conv(ring_, m, period, b_next, slot):
                out = u[slot][:, m, :]
                h_ = hid[m % 2]
                nc.vector.tensor_copy(h_[:, 0:3], hist[:, b_next, m, :])
                s_, v = ring_.emptied(("hid", m), period)
                dve.drain()
                dve.wait_ge(s_, v)
                nc.vector.tensor_copy(hist[:, b_next, m, :], h_[:, T:T + 3])
                nc.vector.tensor_scalar(out, h_[:, 0:T], ch[:, m, 0:1], ch[:, m, 4:5], ALU.mult, ALU.add)
                for tap in range(1, 4):
                    dve.drain()
                    last_ = nc.vector.scalar_tensor_tensor(out, h_[:, tap:tap + T], ch[:, m, tap:tap + 1], out,
                                                           ALU.mult, ALU.add)
                last_.then_inc(conv_done, 1)

            def ssm_sums(c_next):
                wait(dve, sq_ready, 2 * (c_next + 1))
                nc.vector.tensor_reduce(ssq[:, :, 0], ssm[:, :, 0:RANK], AX.X, ALU.add)
                nc.vector.tensor_reduce(ssq[:, :, 1:3], ssm[:, :, RANK:].rearrange("p j (q n) -> p j q n", q=2),
                                        AX.X, ALU.add)
                dve.drain()
                nc.vector.tensor_scalar(ssq[:, :, 0], ssq[:, :, 0], 1.0 / RANK, SSM_EPS, ALU.mult, ALU.add)
                nc.vector.tensor_scalar(ssq[:, :, 1:3], ssq[:, :, 1:3], 1.0 / NSTATE, SSM_EPS, ALU.mult, ALU.add)
                dve.drain().then_inc(ssq_ready, 1)

            def ssm_norm(ring_, c_next):
                wait(dve, rssm_ready, c_next + 1)
                for n in range(2):
                    bank = PJ[ring_.bank(("xp", n))][:, 0:2 * SP_].rearrange("p (j n) -> p j n", j=2)
                    nc.vector.tensor_tensor(ssm[:, 2 * n:2 * n + 2, 0:RANK], bank[:, :, 0:RANK],
                                            rssm[:, 2 * n:2 * n + 2, 0:1].to_broadcast([P, 2, RANK]), ALU.mult)
                    for q in range(2):
                        lo = RANK + q * NSTATE
                        last_ = nc.vector.tensor_tensor(
                            ssm[:, 2 * n:2 * n + 2, lo:lo + NSTATE], bank[:, :, lo:lo + NSTATE],
                            rssm[:, 2 * n:2 * n + 2, 1 + q:2 + q].to_broadcast([P, 2, NSTATE]), ALU.mult)
                    last_.then_inc(ring_.taken["dve"], 1)

            def dt_floor(ring_, h, period):
                s_, v = ring_.emptied((f"dt{h}", GH - 1), period)
                dve.wait_ge(s_, v)
                nc.vector.tensor_scalar_min(xt[:], dt[h][:], 30.0).then_inc(dt_min, 1)

            def dt_max(h, n):
                dve.wait_ge(dt_log, n + 1)
                nc.vector.tensor_tensor(dt[h][:], dt[h][:], xt[:], ALU.max).then_inc(dt_ready, 1)

            def add_res(ring_, j, period, c_prev):
                dve.wait_ge(ring_.full, ring_.filled(("out", j), period))
                wait(dve, res_loaded[j % 2], 16 * (c_prev * 2 + j // 2 + 1))
                nc.vector.tensor_tensor(res[j % 2][:], PJ[ring_.bank(("out", j))][:], res[j % 2][:], ALU.add
                                        ).then_inc(x1_ready, 1)
                dve.wait_ge(x1_ready, c_prev * NT + j + 1)
                dve.sem_inc(ring_.taken["dve"], 1)

            def y_half(h, c, slot):
                dve.wait_ge(sum_done, c * U + NSTATE * (h + 1))
                for g in range(GH):
                    nc.vector.scalar_tensor_tensor(u[slot][:, GH * h + g, :], u[slot][:, GH * h + g, :],
                                                   ch[:, GH * h + g, 5:6], Y[g][:], ALU.mult, ALU.add
                                                   ).then_inc(y_taken, 1)

            def y_gate(h, c, slot):
                wait(dve, gate_ready, c + 1)
                dve.wait_ge(y_taken, (2 * c + h + 1) * GH)
                part = slice(GH * h, GH * h + GH)
                nc.vector.tensor_tensor(u[slot][:, part, :], u[slot][:, part, :], gate[:, part, :], ALU.mult
                                        ).then_inc(y_ready, 1)

            dve.wait_ge(w_loaded, 16 * (KB + 5))
            dve.wait_ge(consts_ready, 2)
            ln_stats(0)
            ln_apply(0)
            for m in range(G):
                conv(ahead, m, 0, 0, 0)
            ssm_sums(0)
            ssm_norm(ahead, 0)
            dve.drain().then_inc(ssm_ready, 1)
            dt_floor(ahead, 0, 0)
            dt_max(0, 0)

            def body(i, b, c, first, last):
                def piece(k):
                    if k == 2 and not last:
                        ln_stats(c + 1)
                    if k == 4 and not last:
                        ln_apply(c + 1)
                    if k == 10:
                        dt_floor(steady, 1, c)
                    if k == 11:
                        dt_max(1, 2 * c + 1)
                    for j in range(NT):
                        if UNIT_OF[("out", j, 1)] == k:
                            if first:
                                dve.drain().then_inc(steady.taken["dve"], 1)
                            else:
                                add_res(steady, j, c, c - 1)
                    if not last:
                        for kind, m, _ in (blocks(k - 1) if 1 <= k < 19 else ()):
                            if kind == "hid":
                                conv(steady, m, c, 1 - b, 1 - b)
                        if k == 22:
                            ssm_sums(c + 1)
                        if k == 23:
                            ssm_norm(steady, c + 1)
                            dve.drain().then_inc(ssm_ready, 1)
                        if k == 27:
                            dt_floor(steady, 0, c)
                        if k == 28:
                            dt_max(0, 2 * c + 2)
                    if k == 15:
                        y_half(0, c, b)
                    if k == 20:
                        y_gate(0, c, b)
                    if k == U - 1:
                        y_half(1, c, b)
                        y_gate(1, c, b)

                for k in range(U):
                    wait(dve, dbu_ready, c * U + k + 1)
                    wait(dve, sum_done, c * U + k - 1)
                    for g in range(GH):
                        wait(dve, da_ready, GH * (c * U + k) + g + 1)
                        nc.vector.tensor_tensor_scan(s[k % 2][:, g, :], DA[g % 2][:], dbu[k % 2][:, g, :],
                                                     state[:, b, k, g:g + 1], ALU.mult, ALU.add
                                                     ).then_inc(scan_done, 1)
                    wait(dve, scan_done, GH * (c * U + k + 1))
                    nc.vector.tensor_copy(state[:, b, k, :], s[k % 2][:, :, T - 1]).then_inc(state_saved, 1)
                    wait(dve, c_loaded[k % 2], 16 * (c * (U // 2) + k // 2 + 1))
                    wait(dve, state_saved, c * U + k + 1)
                    nc.vector.tensor_tensor(s[k % 2][:], s[k % 2][:], Cb[k % 2][:].unsqueeze(1).to_broadcast([P, GH, T]),
                                            ALU.mult).then_inc(z_ready, 1)
                    piece(k)

            periods(dve, body)
            for j in range(NT):
                add_res(after, j, 0, NCH - 1)

        @block.tensor
        def _(pe):
            def bank_of(ring_, use, period):
                sem_, value = ring_.before(use, period)
                wait(pe, sem_, value)
                return PJ[ring_.bank(use)]

            def turn_x(ring_, period, c_next):
                wait(pe, xn_ready, c_next + 1)
                for kb in range(KB):
                    bank = bank_of(ring_, ("xT", kb), period)
                    for j in range(NT):
                        last_ = nc.tensor.transpose(bank[:, j * P:(j + 1) * P], xt[:, j, kb * P:(kb + 1) * P], ident[:])
                    last_.then_inc(ring_.full, 1)

            def project(ring_, use, period, lo):
                bank = bank_of(ring_, use, period)
                for kb in range(KB):
                    last_ = nc.tensor.matmul(bank[:], w_in[:, kb, lo:lo + P], xnT[:, kb, :],
                                             start=(kb == 0), stop=(kb == KB - 1))
                last_.then_inc(ring_.full, 1)

            def x_proj(ring_, n, period, c_next, slot):
                wait(pe, u_ready, c_next + 1)
                bank = bank_of(ring_, ("xp", n), period)
                for j in range(2):
                    for g in range(G):
                        t0 = (2 * n + j) * P
                        last_ = nc.tensor.matmul(bank[:, j * SP_:(j + 1) * SP_], u[slot][:, g, t0:t0 + P],
                                                 w_xp[:, g, :], start=(g == 0), stop=(g == G - 1))
                last_.then_inc(ring_.full, 1)

            def turn_ssm(ring_, period, c_next):
                wait(pe, ssm_ready, c_next + 1)
                bank = bank_of(ring_, ("turn", 0), period)
                for j in range(NT):
                    last_ = nc.tensor.transpose(bank[:, j * P:(j + 1) * P], ssm[:, j, 0:RANK], ident[:])
                last_.then_inc(ring_.full, 1)
                bank = bank_of(ring_, ("turn", 1), period)
                for j in range(NT):
                    last_ = nc.tensor.transpose(bank[0:2 * NSTATE, j * P:(j + 1) * P], ssm[:, j, RANK:], ident[:])
                last_.then_inc(ring_.full, 1)

            def dt_proj(ring_, h, g, period):
                sem_, value = ring_.emptied(("turn", 0), period)
                if h == 0:
                    pe.wait_ge(sem_, value)
                bank = bank_of(ring_, (f"dt{h}", g), period)
                lo = (GH * h + g) * P
                nc.tensor.matmul(bank[:], w_dt[:, lo:lo + P], dtnT[:], start=True, stop=True).then_inc(ring_.full, 1)

            def out_proj(ring_, j, part, period, slot):
                bank = bank_of(ring_, ("out", j), period) if part == 0 else PJ[ring_.bank(("out", j))]
                for g in range(GH * part, GH * part + GH):
                    last_ = nc.tensor.matmul(bank[:], u[slot][:, g, j * P:(j + 1) * P], w_out[:, g, :],
                                             start=(g == 0), stop=(g == G - 1))
                if part == 1:
                    last_.then_inc(ring_.full, 1)

            pe.wait_ge(w_loaded, 16 * (KB + 5))
            turn_x(ahead, 0, 0)
            pe.wait_ge(ahead.taken["act"], KB)
            for m in range(G):
                project(ahead, ("hid", m), 0, m * P)
            for n in range(2):
                x_proj(ahead, n, 0, 0, 0)
            turn_ssm(ahead, 0, 0)
            for g in range(GH):
                dt_proj(ahead, 0, g, 0)
            pe.wait_ge(ahead.taken["act"], ahead.per["act"])

            def body(i, b, c, first, last):
                def pieces(k):
                    if k == K_XT:
                        if last:
                            pe.drain().then_inc(steady.full, KB)
                        else:
                            turn_x(steady, c, c + 1)
                    if k in K_DT1:
                        for g in ((0, 1) if k == K_DT1[0] else (2, 3)):
                            dt_proj(steady, 1, g, c)
                    for kind, m, part in (blocks(k) if k < 18 else ()):
                        if kind == "gate":
                            project(steady, ("gate", m), c, INTER + m * P)
                        if kind == "out":
                            if first:
                                if part == 0:
                                    pe.drain().then_inc(steady.full, 1)
                            else:
                                if m == 0 and part == 0:
                                    pe.wait_ge(y_ready, 2 * c)
                                out_proj(steady, m, part, c, 1 - b)
                        if kind == "hid" and not last:
                            if m == 0:
                                pe.wait_ge(*steady.emptied(("xT", KB - 1), c))
                            project(steady, ("hid", m), c, m * P)
                    if last:
                        return
                    if k in K_XP:
                        x_proj(steady, k - K_XP[0], c, c + 1, 1 - b)
                    if k == K_TURN:
                        turn_ssm(steady, c, c + 1)
                    if k in K_DT0:
                        for g in ((0, 1) if k == K_DT0[0] else (2, 3)):
                            dt_proj(steady, 0, g, c)

                for k in range(U):
                    pieces(k)
                    h, n = k // NSTATE, k % NSTATE
                    if n == 0:
                        wait(pe, y_taken, (2 * c + h) * GH)
                    pe.wait_ge(z_ready, c * U + k + 1)
                    for g in range(GH):
                        last_ = nc.tensor.matmul(Y[g][:], ident[:], s[k % 2][:, g, :],
                                                 start=(n == 0), stop=(n == NSTATE - 1))
                    last_.then_inc(sum_done, 1)

            periods(pe, body)
            pe.wait_ge(y_ready, 2 * NCH)
            for j in range(NT):
                for part in range(2):
                    if part == 0 and j >= 2:
                        pe.wait_ge(after.taken["dve"], j - 1)
                    bank = PJ[after.bank(("out", j))]
                    for g in range(GH * part, GH * part + GH):
                        last_ = nc.tensor.matmul(bank[:], u[1][:, g, j * P:(j + 1) * P], w_out[:, g, :],
                                                 start=(g == 0), stop=(g == G - 1))
                last_.then_inc(after.full, 1)



def blocks_after(nc, x1, w, out):
    BATCH, SEQ, HID = x1.shape
    KB = HID // P
    RANKS = w["factors"].shape[0]
    TILES = BATCH * SEQ // P
    HEADS, HD = 16, 32
    HG = HEADS * HD // P
    ROT = 8
    NTILE, DS, GRID = w["slopes"].shape
    NCL = NTILE // 8
    BIG = 1e30
    RMS_EPS = 1e-5
    x1_v = x1.rearrange("b (i p) d -> b i p d", p=P)
    out_v = out.rearrange("b (i p) d -> b i p d", p=P)
    LAST_STAGE = 6

    ctx = ExitStack()
    with ctx:
        def sb(name, shape, dt=F32):
            return ctx.enter_context(nc.sbuf_tensor(name, shape, dt))

        def sem(name):
            return ctx.enter_context(nc.semaphore(name))

        w_f = sb("w_f", [P, KB, HID])
        w_part = [sb(f"w_part{i}", [P, KB, HID]) for i in range(2)]
        w_q, w_k, w_v, w_o = (sb(n, [P, KB, HID]) for n in ("w_q", "w_k", "w_v", "w_o"))
        rms_w = sb("rms_w", [P, KB])
        ident = sb("ident2", [P, P])
        ones = sb("ones", [P, P])
        decay = sb("decay", [P, 4, HG, P])
        q_dec = sb("q_dec", [P, HG, P])
        k_dec = sb("k_dec", [P, HEADS])
        kv_dec = sb("kv_dec", [P, HG, P])
        kv_mask = sb("kv_mask", [P, HG, P])
        bias_b = sb("bias_b", [P, HID])
        gamma_b = sb("gamma_b", [P, HID])
        beta_b = sb("beta_b", [P, HID])
        sign_b = sb("sign_b", [P, HID], BF16)
        tie8 = sb("tie8", [P, 8])
        tie64 = sb("tie64", [P, NTILE])
        grid16 = sb("grid16", [P, GRID])
        tab = sb("tab", [NTILE, 2, DS * GRID])
        oscale = sb("oscale", [NTILE, 1])
        smean = sb("smean", [NTILE, DS])
        sdiag = sb("sdiag", [NTILE, NTILE, DS])

        x1t = [sb(f"x1t{i}", [P, HID]) for i in range(2)]
        rot = [sb(f"rot{i}", [P, 2, 2 * ROT]) for i in range(2)]
        xa = [sb(f"xa{i}", [P, HID]) for i in range(2)]
        xaT = sb("xaT", [P, KB, P])
        x2 = [sb(f"x2_{i}", [P, HID]) for i in range(4)]
        xb = [sb(f"xb{i}", [P, HID]) for i in range(2)]
        xbT = sb("xbT", [P, KB, P])
        qk = [sb(f"qk{i}", [P, 2, HID]) for i in range(2)]
        rc = sb("rc", [P, 2 * HEADS, 2, ROT])
        rs_ = sb("rs", [P, 2 * HEADS, 2, ROT])
        vv = [sb(f"vv{i}", [P, HID]) for i in range(2)]
        kd = [sb(f"kd{i}", [P, HID]) for i in range(2)]
        qTs = sb("qTs", [P, HG, P])
        qdT = sb("qdT", [P, HG, P])
        kTs = sb("kTs", [P, HG, P])
        scm = sb("scm", [P, 4, HG, P])
        kv = [sb(f"kv{i}", [P, HG, P]) for i in range(BATCH)]
        kvd = sb("kvd", [P, HG, P])
        kvu = sb("kvu", [P, HG, P])
        at_s = [sb(f"at_s{i}", [P, HID]) for i in range(2)]
        junk = sb("junk", [P, HID])
        rsum = [sb(f"rsum{i}", [P, 1]) for i in range(2)]
        rrms = [sb(f"rrms{i}", [P, 1]) for i in range(2)]
        aTs = sb("aTs", [P, KB, P])
        x3 = [sb(f"x3_{i}", [P, HID]) for i in range(2)]
        x3n = [sb(f"x3n{i}", [P, HID]) for i in range(2)]
        r_t = [sb(f"r_t{i}", [P, HID]) for i in range(2)]
        xf = [sb(f"xf{i}", [P, HID]) for i in range(2)]
        sg = [sb(f"sg{i}", [P, HID], BF16) for i in range(2)]
        pr = sb("pr", [P, HID], BF16)
        xm = sb("xm", [P, NTILE, DS])
        ts = sb("ts", [P, NTILE])
        cs = sb("cs", [P, 8])
        cm = sb("cm", [P, 8])
        top = sb("top", [P, 2])
        tk = sb("tk", [P, 2])
        pen = sb("pen", [P, NTILE])
        cand = sb("cand", [P, 2, NTILE])
        acc = sb("acc", [P, 2, NTILE])
        ohx = [sb(f"ohx{i}", [P, NTILE + DS]) for i in range(2)]
        ln = {n: (sb(f"st_{n}", [P, 6]), sb(f"mv_{n}", [P, 2]), sb(f"sd_{n}", [P, 1]), sb(f"rd_{n}", [P, 1]))
              for n in ("a", "b", "c", "d")}
        banks = [ctx.enter_context(nc.psum_tensor(f"bank{i}", [P, HID], F32)) for i in range(8)]
        ohx_d = nc.dram_tensor("ohx_d", (TILES, P, NTILE + DS), F32, kind="Internal").ap()

        USES = [("xT", 1), ("x2T", 2), ("aT", 4), ("qT", 3), ("kT", 3), ("ffn", 1), ("q", 2), ("k", 2), ("v", 2),
                ("sc0", 3), ("sc1", 3), ("sc2", 3), ("sc3", 3), ("wo", 4), ("kvu", 3), ("at", 3)]
        AT = {n: p for p, (n, _) in enumerate(USES)}
        filled = {n: sem(f"filled_{n}") for n, _ in USES}
        taken = {n: sem(f"taken_{n}") for n, _ in USES}

        def bank(name):
            return banks[AT[name] % 8]

        def num(t):
            return t[1] if t[0] is None else t[0] * 4 + t[1]

        def back(t, n):
            return (t[0], t[1] - n)

        def valid(t):
            return t[0] is not None or 0 <= t[1] < TILES

        def where(t):
            b = t[1] % 2
            i = (t[1] - b) // 2
            return b, (i if t[0] is None else t[0] * 2 + i)

        def stored_count(a):
            b = a[1] % 2
            n = (a[1] - b) // 2
            return n if a[0] is None else a[0] * 2 + n

        def user_before(name, step):
            p = AT[name]
            while True:
                p, step = (p - 8, step) if p >= 8 else (p + 8, back(step, 1))
                if step[0] is None and step[1] < 0:
                    return None
                n, s_ = USES[p]
                if valid(back(step, s_)):
                    return n, back(step, s_)

        names = ("w_loaded2", "f_loaded0", "f_loaded1", "f_added", "setup_dve", "setup_act", "setup_pool", "setup_pe",
                 "xa_ready", "x1b_ready", "x2_ready", "xb_ready", "rot_parts", "qk_ready", "kd_ready", "qd_ready",
                 "kvd_ready", "kvu_ready", "kv_ready", "rms_ready", "x3_ready", "x3n_ready", "r_ready",
                 "xf_normed", "xf_scaled", "xf_ready", "sg_ready", "ohx_ready", "scored")
        S = {n: sem(n) for n in names}
        sp_steps, qt_copied = sem("sp_steps2"), sem("qt_copied")
        x1_loaded = [sem(f"x1_loaded{i}") for i in range(2)]
        rot_loaded = [sem(f"rot_loaded{i}") for i in range(2)]
        r_stored = [sem(f"r_stored{i}") for i in range(2)]
        ohx_stored = [sem(f"ohx_stored{i}") for i in range(2)]
        var_ready = {n: sem(f"var_ready_{n}") for n in ln}
        sd_ready = {n: sem(f"sd_ready_{n}") for n in ln}

        region = ExitStack()
        block = region.enter_context(nc.Block())

        def steps(eng, body):
            for t in range(8):
                body((None, t))
            with eng.Fori(2, TILES // 4) as i:
                for u_ in range(4):
                    body((i, u_))
            for t in range(TILES, TILES + LAST_STAGE):
                body((None, t))

        @block.sync
        def _(sp):
            def held(sem_, value):
                wait(sp, sem_, value)
                sp.sem_inc(sp_steps, 1)

            for n, dst in (("Wq", w_q), ("Wk", w_k), ("Wv", w_v), ("Wo", w_o)):
                sp.dma_start(dst[:], w[n].rearrange("(k p) n -> p k n", p=P)).then_inc(S["w_loaded2"], 16)
            for r in range(RANKS):
                if r >= 2:
                    sp.wait_ge(S["f_added"], r - 1)
                sp.dma_start(w_part[r % 2][:], w["factors"][r].rearrange("(k p) n -> p k n", p=P)
                             ).then_inc(S[f"f_loaded{r % 2}"], 16)

            def body(t):
                a = t
                if valid(a):
                    s_ = a[1] % 2
                    b, i = where(a)
                    held(S["x2_ready"], num(a) - 1)
                    sp.dma_start(x1t[s_][:], x1_v[b, i]).then_inc(x1_loaded[s_], 16)
                a = back(t, 1)
                if valid(a):
                    s_ = a[1] % 2
                    b, i = where(a)
                    held(S["rot_parts"], num(a) - 1)
                    sp.dma_start(rot[s_][:], w["rot"][i]).then_inc(rot_loaded[s_], 16)
                a = back(t, 6)
                if valid(a):
                    s_ = a[1] % 2
                    b, i = where(a)
                    held(S["r_ready"], num(a) + 1)
                    sp.dma_start(out_v[b, i], r_t[s_][:]).then_inc(r_stored[s_], 16)
                    held(S["ohx_ready"], num(a) + 1)
                    sp.dma_start(ohx_d[num(a)], ohx[s_][:]).then_inc(ohx_stored[s_], 16)

            steps(sp, body)
            for s_ in range(2):
                sp.wait_ge(r_stored[s_], 16 * TILES // 2)
                sp.wait_ge(ohx_stored[s_], 16 * TILES // 2)

        @block.gpsimd
        def _(pool):
            nc.gpsimd.memset(ones[:], 1.0)
            nc.gpsimd.memset(kv[0][:], 0.0)
            nc.gpsimd.memset(kv[1][:], 0.0)
            nc.gpsimd.memset(acc[:], -BIG)
            pool.drain().then_inc(S["setup_pool"], 1)
            pool.wait_ge(S["setup_act"], 1)

            def body(t):
                a = back(t, 5)
                if valid(a):
                    s_ = a[1] % 2
                    wait(pool, S["x3n_ready"], num(a) + 1)
                    if a[0] is not None or a[1] >= 2:
                        pool.wait_ge(r_stored[s_], 16 * stored_count(a))
                    nc.gpsimd.tensor_tensor(r_t[s_][:], x3[s_][:], x3n[s_][:], ALU.add).then_inc(S["r_ready"], 1)
                a = t
                if valid(a):
                    s_ = a[1] % 2
                    wait(pool, S["xa_ready"], num(a) + 1)
                    nc.gpsimd.tensor_tensor(x1t[s_][:], x1t[s_][:], bias_b[:], ALU.add).then_inc(S["x1b_ready"], 1)
                a = back(t, 5)
                if valid(a):
                    s_ = a[1] % 2
                    wait(pool, S["xf_normed"], num(a) + 1)
                    nc.gpsimd.tensor_tensor(xf[s_][:], xf[s_][:], gamma_b[:], ALU.mult).then_inc(S["xf_scaled"], 1)
                    wait(pool, S["xf_scaled"], num(a) + 1)
                    nc.gpsimd.tensor_tensor(xf[s_][:], xf[s_][:], beta_b[:], ALU.add).then_inc(S["xf_ready"], 1)
                a = back(t, 2)
                if valid(a):
                    s_ = a[1] % 2
                    wait(pool, S["rot_parts"], num(a) + 1)
                    turned = qk[s_][:].rearrange("p q (h z j) -> p (q h) z j", h=HEADS, z=2)[:, :, :, 0:ROT]
                    nc.gpsimd.tensor_tensor(turned, rc[:], rs_[:], ALU.add).then_inc(S["qk_ready"], 1)
                    wait(pool, S["qk_ready"], num(a) + 1)
                    wait(pool, filled["kvu"], num(a) - 1)
                    nc.gpsimd.tensor_tensor(kd[s_][:].rearrange("p (h d) -> p h d", h=HEADS),
                                            qk[s_][:, 1, :].rearrange("p (h d) -> p h d", h=HEADS),
                                            k_dec[:].unsqueeze(2).to_broadcast([P, HEADS, HD]), ALU.mult
                                            ).then_inc(S["kd_ready"], 1)
                a = back(t, 3)
                if valid(a):
                    b = a[1] % 2
                    wait(pool, S["kv_ready"], num(a))
                    nc.gpsimd.tensor_tensor(kvd[:], kv[b][:], kv_dec[:], ALU.mult).then_inc(S["kvd_ready"], 1)
                    wait(pool, S["kvd_ready"], num(a) + 1)
                    wait(pool, S["kvu_ready"], num(a) + 1)
                    wait(pool, filled["at"], num(a) + 1)
                    nc.gpsimd.tensor_tensor(kv[b][:], kvd[:], kvu[:], ALU.add).then_inc(S["kv_ready"], 1)

            steps(pool, body)

        @block.scalar
        def _(act):
            for dst, src in ((rms_w, w["rms_w"]), (ident, w["eye"]), (decay, w["decay"]), (q_dec, w["q_dec"]),
                             (k_dec, w["k_dec"]), (kv_dec, w["kv_dec"]), (kv_mask, w["kv_mask"]),
                             (tie8, w["tie8"]), (tie64, w["tie64"]), (grid16, w["grid16"]), (oscale, w["oscale"])):
                act.dma_start(dst[:], src).then_inc(S["w_loaded2"], 16)
            for dst, src in ((bias_b, w["bias"]), (gamma_b, w["gamma"]), (beta_b, w["beta"])):
                act.dma_start(dst[:], src.to_broadcast([P, HID])).then_inc(S["w_loaded2"], 16)
            act.dma_start(tab[:, 0, :], w["bases"].rearrange("a j g -> a (j g)")).then_inc(S["w_loaded2"], 16)
            act.dma_start(tab[:, 1, :], w["slopes"].rearrange("a j g -> a (j g)")).then_inc(S["w_loaded2"], 16)
            act.wait_ge(S["setup_dve"], 1)
            nc.scalar.activation(smean[:], smean[:], ACT.Sign).then_inc(S["setup_act"], 1)
            act.wait_ge(S["setup_pe"], 1)
            nc.scalar.copy(sign_b[:], banks[0][:]).then_inc(S["setup_act"], 1)

            def take(name, a, dst, view=lambda p: p[:]):
                act.wait_ge(filled[name], num(a) + 1)
                nc.scalar.copy(dst, view(bank(name))).then_inc(taken[name], 1)

            def root(n, a, lag):
                wait(act, var_ready[n], num(a) + 1)
                nc.scalar.activation(ln[n][2][:], ln[n][1][:, 1:2], ACT.Sqrt, bias=LN_EPS).then_inc(sd_ready[n], 1)

            flat = "p (k n) -> p k n"

            def body(t):
                if valid(back(t, 1)):
                    a = back(t, 1)
                    wait(act, filled["ffn"], num(a))
                    take("xT", a, xaT[:].rearrange("p k n -> p (k n)"))
                if valid(back(t, 2)):
                    a = back(t, 2)
                    wait(act, filled["v"], num(a))
                    take("x2T", a, xbT[:].rearrange("p k n -> p (k n)"))
                if valid(back(t, 5)):
                    root("c", back(t, 5), 5)
                if valid(back(t, 4)):
                    a = back(t, 4)
                    wait(act, filled["wo"], num(a))
                    take("aT", a, aTs[:].rearrange("p k n -> p (k n)"))
                if valid(back(t, 3)):
                    a = back(t, 3)
                    wait(act, filled["sc3"], num(a))
                    act.wait_ge(filled["qT"], num(a) + 1)
                    nc.scalar.copy(qTs[:].rearrange("p k n -> p (k n)"), bank("qT")[:]).then_inc(qt_copied, 1)
                    take("kT", a, kTs[:].rearrange("p k n -> p (k n)"))
                if valid(t):
                    root("a", t, 0)
                if valid(back(t, 5)):
                    root("d", back(t, 5), 5)
                if valid(back(t, 2)):
                    a = back(t, 2)
                    s_ = a[1] % 2
                    wait(act, filled["kT"], num(a) - 1)
                    wait(act, S["kd_ready"], num(a) - 1)
                    take("q", a, qk[s_][:, 0, :])
                    take("k", a, qk[s_][:, 1, :])
                    wait(act, filled["at"], num(a) - 1)
                    take("v", a, vv[s_][:])
                if valid(back(t, 1)):
                    root("b", back(t, 1), 1)
                if valid(back(t, 5)):
                    a = back(t, 5)
                    wait(act, S["xf_ready"], num(a) + 1)
                    wait(act, S["scored"], num(a) - 1)
                    nc.scalar.activation(sg[a[1] % 2][:], xf[a[1] % 2][:], ACT.Sign).then_inc(S["sg_ready"], 1)
                if valid(back(t, 3)):
                    a = back(t, 3)
                    s_ = a[1] % 2
                    act.drain()
                    act.wait_ge(filled["at"], num(a) + 1)
                    wait(act, S["x3_ready"], num(a) - 1)
                    nc.scalar.activation(junk[:], bank("at")[:], ACT.Square, accum_out=rsum[s_][:])
                    nc.scalar.copy(at_s[s_][:], bank("at")[:])
                    act.drain().then_inc(taken["at"], 1)
                    nc.scalar.activation(rsum[s_][:], rsum[s_][:], ACT.Sqrt, bias=RMS_EPS, scale=1.0 / HID
                                         ).then_inc(S["rms_ready"], 1)

            steps(act, body)

        @block.vector
        def _(dve):
            dve.wait_ge(S["w_loaded2"], 16 * 20)
            dve.wait_ge(S["setup_pool"], 1)
            nc.vector.tensor_reduce(smean[:], tab[:, 1, :].rearrange("a (j g) -> a j g", g=GRID), AX.X, ALU.add
                                    ).then_inc(S["setup_dve"], 1)
            dve.wait_ge(S["setup_act"], 1)
            nc.vector.tensor_tensor(sdiag[:], ident[0:NTILE, 0:NTILE].unsqueeze(2).to_broadcast([NTILE, NTILE, DS]),
                                    smean[:].unsqueeze(1).to_broadcast([NTILE, NTILE, DS]), ALU.mult
                                    ).then_inc(S["setup_dve"], 1)
            for k in range(KB):
                nc.vector.tensor_scalar(w_o[:, k, :], w_o[:, k, :], rms_w[:, k:k + 1], None, ALU.mult)
            nc.vector.tensor_scalar(tab[:], tab[:], oscale[:], None, ALU.mult)
            for r in range(RANKS):
                dve.wait_ge(S[f"f_loaded{r % 2}"], 16 * (r // 2 + 1))
                if r == 0:
                    nc.vector.tensor_copy(w_f[:], w_part[0][:]).then_inc(S["f_added"], 1)
                else:
                    dve.wait_ge(S["f_added"], r)
                    nc.vector.tensor_tensor(w_f[:], w_f[:], w_part[r % 2][:], ALU.add).then_inc(S["f_added"], 1)
            dve.drain().then_inc(S["setup_dve"], 1)
            dve.wait_ge(S["setup_act"], 2)

            def stats(n, x_):
                nc.vector.bn_stats(ln[n][0][:], x_)
                dve.drain()
                nc.vector.bn_aggr(ln[n][1][:], ln[n][0][:]).then_inc(var_ready[n], 1)

            def norm(n, a, x_, dst, done):
                dve.wait_ge(sd_ready[n], num(a) + 1)
                nc.vector.reciprocal(ln[n][3][:], ln[n][2][:])
                dve.drain()
                nc.vector.tensor_scalar(dst, x_, ln[n][1][:, 0:1], ln[n][3][:], ALU.subtract, ALU.mult).then_inc(done, 1)

            def score(a):
                s_ = a[1] % 2
                oh = ohx[s_][:, 0:NTILE]
                xs = ohx[s_][:, NTILE:NTILE + DS]
                dve.wait_ge(S["sg_ready"], num(a) + 1)
                nc.vector.tensor_tensor(pr[:], sg[s_][:], sign_b[:], ALU.mult)
                dve.drain()
                nc.vector.tensor_reduce(ts[:], pr[:].rearrange("p (i j) -> p i j", j=DS), AX.X, ALU.add)
                dve.drain()
                nc.vector.tensor_reduce(cs[:], ts[:].rearrange("p (c i) -> p c i", c=NCL), AX.X, ALU.add)
                dve.drain()
                nc.vector.scalar_tensor_tensor(cs[:], cs[:], 8.0, tie8[:], ALU.mult, ALU.add)
                nc.vector.scalar_tensor_tensor(ts[:], ts[:], 8.0, tie64[:], ALU.mult, ALU.add)
                dve.drain()
                nc.vector.tensor_reduce(top[:, 0:1], cs[:], AX.X, ALU.max)
                dve.drain()
                nc.vector.tensor_scalar(cm[:], cs[:], top[:, 0:1], 1024.0, ALU.is_equal, ALU.mult)
                dve.drain()
                nc.vector.tensor_tensor(ts[:].rearrange("p (c i) -> p c i", c=NCL),
                                        ts[:].rearrange("p (c i) -> p c i", c=NCL),
                                        cm[:].unsqueeze(2).to_broadcast([P, NCL, 8]), ALU.add)
                dve.drain()
                nc.vector.tensor_reduce(top[:, 1:2], ts[:], AX.X, ALU.max)
                if a[0] is not None or a[1] >= 2:
                    dve.drain()
                    dve.wait_ge(ohx_stored[s_], 16 * stored_count(a))
                else:
                    dve.drain()
                nc.vector.tensor_scalar(oh, ts[:], top[:, 1:2], None, ALU.is_equal)
                dve.drain()
                nc.vector.tensor_tensor(xm[:], xf[s_][:].rearrange("p (i j) -> p i j", j=DS),
                                        oh.unsqueeze(2).to_broadcast([P, NTILE, DS]), ALU.mult)
                nc.vector.tensor_scalar(pen[:], oh, -1.0, BIG, ALU.add, ALU.mult)
                dve.drain()
                nc.vector.tensor_reduce(xs, xm[:].rearrange("p i j -> p j i"), AX.X, ALU.add)
                dve.drain()
                nc.vector.tensor_reduce(tk[:, 0:1], xs, AX.X, ALU.max)
                nc.vector.tensor_reduce(tk[:, 1:2], xs, AX.X, ALU.min, negate=True)
                dve.drain()
                for q in range(2):
                    nc.vector.scalar_tensor_tensor(cand[:, q, :], oh, tk[:, q:q + 1], pen[:], ALU.mult, ALU.add)
                dve.drain().then_inc(S["ohx_ready"], 1)
                nc.vector.tensor_tensor(acc[:], acc[:], cand[:], ALU.max).then_inc(S["scored"], 1)

            def body(t):
                s5, s3, s2, s1, s4 = back(t, 5), back(t, 3), back(t, 2), back(t, 1), back(t, 4)
                if valid(s5):
                    stats("c", x3[s5[1] % 2][:])
                if valid(s3):
                    dve.wait_ge(filled["qT"], num(s3) + 1)
                    dve.wait_ge(qt_copied, num(s3) + 1)
                    wait(dve, filled["at"], num(s3))
                    nc.vector.tensor_tensor(qdT[:].rearrange("p k n -> p (k n)"), bank("qT")[:],
                                            q_dec[:].rearrange("p k n -> p (k n)"), ALU.mult).then_inc(taken["qT"], 1)
                if valid(t):
                    dve.wait_ge(x1_loaded[t[1] % 2], 16 * (stored_count(t) + 1))
                    stats("a", x1t[t[1] % 2][:])
                if valid(s5):
                    s_ = s5[1] % 2
                    wait(dve, S["r_ready"], num(s5) - 1)
                    norm("c", s5, x3[s_][:], x3n[s_][:], S["x3n_ready"])
                    dve.drain()
                    stats("d", x3n[s_][:])
                if valid(back(t, 6)):
                    score(back(t, 6))
                if valid(t):
                    wait(dve, filled["xT"], num(t) - 1)
                    norm("a", t, x1t[t[1] % 2][:], xa[t[1] % 2][:], S["xa_ready"])
                if valid(s5):
                    norm("d", s5, x3n[s5[1] % 2][:], xf[s5[1] % 2][:], S["xf_normed"])
                if valid(s1):
                    dve.wait_ge(filled["ffn"], num(s1) + 1)
                    dve.wait_ge(S["x1b_ready"], num(s1) + 1)
                    nc.vector.scalar_tensor_tensor(x2[s1[1] % 4][:], bank("ffn")[:], float(RANKS) ** -0.5,
                                                   x1t[s1[1] % 2][:], ALU.mult, ALU.add)
                    dve.drain().then_inc(taken["ffn"], 1)
                    nc.vector.bn_stats(ln["b"][0][:], x2[s1[1] % 4][:]).then_inc(S["x2_ready"], 1)
                    dve.drain()
                    nc.vector.bn_aggr(ln["b"][1][:], ln["b"][0][:]).then_inc(var_ready["b"], 1)
                if valid(s2):
                    s_ = s2[1] % 2
                    dve.wait_ge(taken["k"], num(s2) + 1)
                    dve.wait_ge(rot_loaded[s_], 16 * (stored_count(s2) + 1))
                    wait(dve, S["qk_ready"], num(s2))
                    pairs = qk[s_][:].rearrange("p q (h z j) -> p (q h) z j", h=HEADS, z=2)[:, :, :, 0:ROT]
                    cos = rot[s_][:, 0, :].rearrange("p (z j) -> p z j", z=2)
                    sin = rot[s_][:, 1, :].rearrange("p (z j) -> p z j", z=2)
                    nc.vector.tensor_tensor(rc[:], pairs, cos.unsqueeze(1).to_broadcast([P, 2 * HEADS, 2, ROT]), ALU.mult)
                    for z in range(2):
                        last_ = nc.vector.tensor_tensor(
                            rs_[:, :, z, :], pairs[:, :, 1 - z, :],
                            sin[:, z, :].unsqueeze(1).to_broadcast([P, 2 * HEADS, ROT]), ALU.mult)
                    dve.drain().then_inc(S["rot_parts"], 1)
                if valid(s1):
                    wait(dve, filled["x2T"], num(s1) - 1)
                    norm("b", s1, x2[s1[1] % 4][:], xb[s1[1] % 2][:], S["xb_ready"])
                if valid(s3):
                    wait(dve, filled["at"], num(s3))
                    for r in range(4):
                        dve.wait_ge(filled[f"sc{r}"], num(s3) + 1)
                        nc.vector.tensor_tensor(scm[:, r, :, :].rearrange("p k n -> p (k n)"), bank(f"sc{r}")[:],
                                                decay[:, r, :, :].rearrange("p k n -> p (k n)"), ALU.mult
                                                ).then_inc(taken[f"sc{r}"], 1)
                if valid(s4):
                    s_ = s4[1] % 2
                    dve.wait_ge(S["rms_ready"], num(s4) + 1)
                    nc.vector.reciprocal(rrms[s_][:], rsum[s_][:])
                    dve.drain()
                    dve.wait_ge(filled["wo"], num(s4) + 1)
                    wait(dve, S["r_ready"], num(s4) - 1)
                    nc.vector.scalar_tensor_tensor(x3[s_][:], bank("wo")[:], rrms[s_][:], x2[s4[1] % 4][:],
                                                   ALU.mult, ALU.add).then_inc(taken["wo"], 1)
                    dve.drain().then_inc(S["x3_ready"], 1)
                if valid(s3):
                    dve.wait_ge(filled["kvu"], num(s3) + 1)
                    wait(dve, S["kv_ready"], num(s3))
                    nc.vector.tensor_tensor(kvu[:].rearrange("p k n -> p (k n)"), bank("kvu")[:],
                                            kv_mask[:].rearrange("p k n -> p (k n)"), ALU.mult
                                            ).then_inc(taken["kvu"], 1)
                    dve.wait_ge(taken["kvu"], num(s3) + 1)
                    dve.sem_inc(S["kvu_ready"], 1)

            steps(dve, body)

        @block.tensor
        def _(pe):
            pe.wait_ge(S["setup_dve"], 2)
            nc.tensor.matmul(banks[0][:], ones[0:NTILE, :], sdiag[:].rearrange("a i j -> a (i j)"),
                             start=True, stop=True).then_inc(S["setup_pe"], 1)
            pe.wait_ge(S["setup_dve"], 3)
            pe.wait_ge(S["setup_act"], 2)

            def free(name, t):
                before = user_before(name, t)
                if before is not None:
                    pe.wait_ge(taken[before[0]], num(before[1]) + 1)
                return bank(name)

            def turn(name, t, src):
                b_ = free(name, t)
                for k in range(KB):
                    last_ = nc.tensor.transpose(b_[:, k * P:(k + 1) * P], src[:, k * P:(k + 1) * P], ident[:])
                last_.then_inc(filled[name], 1)

            def product(name, t, srcT, wt):
                b_ = free(name, t)
                for k in range(KB):
                    last_ = nc.tensor.matmul(b_[:], srcT[:, k, :], wt[:, k, :], start=(k == 0), stop=(k == KB - 1))
                last_.then_inc(filled[name], 1)

            def body(t):
                s1, s2, s3, s4 = back(t, 1), back(t, 2), back(t, 3), back(t, 4)
                if valid(s1):
                    pe.wait_ge(S["xa_ready"], num(s1) + 1)
                    turn("xT", t, xa[s1[1] % 2])
                if valid(s2):
                    pe.wait_ge(S["xb_ready"], num(s2) + 1)
                    turn("x2T", t, xb[s2[1] % 2])
                if valid(s4):
                    pe.wait_ge(taken["at"], num(s4) + 1)
                    turn("aT", t, at_s[s4[1] % 2])
                if valid(s3):
                    pe.wait_ge(S["qk_ready"], num(s3) + 1)
                    turn("qT", t, qk[s3[1] % 2][:, 0, :])
                    turn("kT", t, qk[s3[1] % 2][:, 1, :])
                if valid(s1):
                    pe.wait_ge(taken["xT"], num(s1) + 1)
                    product("ffn", t, xaT, w_f)
                if valid(s2):
                    pe.wait_ge(taken["x2T"], num(s2) + 1)
                    for name, wt in (("q", w_q), ("k", w_k), ("v", w_v)):
                        product(name, t, xbT, wt)
                if valid(s3):
                    pe.wait_ge(qt_copied, num(s3) + 1)
                    pe.wait_ge(taken["kT"], num(s3) + 1)
                    for r in range(4):
                        free(f"sc{r}", t)
                    for g in range(HG):
                        for r in range(4):
                            rows = slice(HD * r, HD * r + HD)
                            last_ = nc.tensor.matmul(bank(f"sc{r}")[:, g * P:(g + 1) * P], kTs[rows, g, :],
                                                     qTs[rows, g, :], start=True, stop=True,
                                                     tile_position=(HD * r, 0))
                            if g == HG - 1:
                                last_.then_inc(filled[f"sc{r}"], 1)
                if valid(s4):
                    pe.wait_ge(taken["aT"], num(s4) + 1)
                    product("wo", t, aTs, w_o)
                if valid(s3):
                    s_ = s3[1] % 2
                    pe.wait_ge(S["kd_ready"], num(s3) + 1)
                    pe.wait_ge(taken["v"], num(s3) + 1)
                    b_ = free("kvu", t)
                    for g in range(HG):
                        cols = slice(g * P, (g + 1) * P)
                        last_ = nc.tensor.matmul(b_[:, cols], kd[s_][:, cols], vv[s_][:, cols],
                                                 start=(g == 0), stop=(g == HG - 1), skip_group_check=True)
                    last_.then_inc(filled["kvu"], 1)
                    pe.wait_ge(taken["qT"], num(s3) + 1)
                    if s3[0] is not None or s3[1] >= 2:
                        pe.wait_ge(S["kv_ready"], num(s3) - 1)
                    b_ = free("at", t)
                    for g in range(HG):
                        cols = slice(g * P, (g + 1) * P)
                        nc.tensor.matmul(b_[:, cols], qdT[:, g, :], kv[s_][:, g, :], start=(g == 0), stop=False,
                                         skip_group_check=True)
                    for r in range(4):
                        pe.wait_ge(taken[f"sc{r}"], num(s3) + 1)
                        for g in range(HG):
                            cols = slice((4 * g + r) * HD, (4 * g + r + 1) * HD)
                            last_ = nc.tensor.matmul(b_[:, cols], scm[:, r, g, :], vv[s_][:, cols], start=False,
                                                     stop=(r == 3 and g == HG - 1), skip_group_check=True)
                    last_.then_inc(filled["at"], 1)

            steps(pe, body)

        region.close()
        finish(nc, out_v, ohx_d, dict(
            R=w_part, od=w_q, eq=w_k[:, 0, :].rearrange("p (t g) -> p t g", g=GRID), prod=w_v, banks=banks,
            ident=ident, ones=ones, tab=tab, grid16=grid16, acc=acc,
            oq=[sb(f"oq{i}", [P, 4, NTILE + DS]) for i in range(2)], ohTs=sb("ohTs", [NTILE, 4 * P]),
            ext_T=sb("ext_T", [P, 1]), ext_diag=sb("ext_diag", [P, P]), ext=sb("ext", [P, 2, NTILE]),
            e=sb("e", [P, 2, 4]), rdn=sb("rdn", [P, 4]), gi=sb("gi", [P, 4, DS], I32),
            **{n: sb(n, [P, 4, DS]) for n in ("v16", "gf", "gt", "bsel", "ssel")}), NTILE, DS, GRID, TILES)


def finish(nc, out_v, ohx_d, buf, NTILE, DS, GRID, TILES):
    N = 4
    R, od, eq, prod, banks = buf["R"], buf["od"], buf["eq"], buf["prod"], buf["banks"]
    oq, ident, ones, tab, grid16 = buf["oq"], buf["ident"], buf["ones"], buf["tab"], buf["grid16"]
    acc, ext_T, ext_diag, ext = buf["acc"], buf["ext_T"], buf["ext_diag"], buf["ext"]
    ohTs, e, rdn, v16, gi, gf, gt, bsel, ssel = (buf[n] for n in (
        "ohTs", "e", "rdn", "v16", "gi", "gf", "gt", "bsel", "ssel"))
    ctx = ExitStack()
    with ctx:
        def sem(name):
            return ctx.enter_context(nc.semaphore(name))

        ext_step, ext_pe = sem("ext_step"), sem("ext_pe")
        r_loaded = [sem(f"r_loaded{i}") for i in range(2)]
        oq_loaded = [sem(f"oq_loaded{i}") for i in range(2)]
        out_stored = [sem(f"out_stored{i}") for i in range(2)]
        turned, ohT_ready, looked_up, looked_taken = sem("turned3"), sem("ohT_ready"), sem("looked_up"), sem("looked_taken")
        od_ready, out_ready, sp_steps3, pe_steps3 = (
            sem("od_ready"), sem("out_ready"), sem("sp_steps3"), sem("pe_steps3"))
        block = ctx.enter_context(nc.Block())
        GROUPS = TILES // N

        def groups(eng, body):
            for v in range(2):
                body(v, v, 0)
            with eng.Fori(1, GROUPS // 2) as i:
                for v in range(2):
                    body(i * 2 + v, v, i)

        @block.sync
        def _(sp):
            def load(G, v, i):
                wait(sp, out_stored[v], i * 32)
                sp.sem_inc(sp_steps3, 1)
                for b in range(2):
                    sp.dma_start(R[v][:, b::2, :], out_v[b, bass.ds(G * 2, 2)].rearrange("i p d -> p i d")
                                 ).then_inc(r_loaded[v], 16)
                sp.dma_start(oq[v][:], ohx_d[bass.ds(G * N, N)].rearrange("t p n -> p t n")).then_inc(oq_loaded[v], 16)

            def store(G, v, i):
                wait(sp, out_ready, G + 1)
                sp.sem_inc(sp_steps3, 1)
                for b in range(2):
                    sp.dma_start(out_v[b, bass.ds(G * 2, 2)].rearrange("i p d -> p i d"), R[v][:, b::2, :]
                                 ).then_inc(out_stored[v], 16)

            load(0, 0, 0)
            load(1, 1, 0)
            with sp.Fori(0, GROUPS // 2 - 1) as i:
                for v in range(2):
                    store(i * 2 + v, v, i)
                    load(i * 2 + (v + 2), v, i + 1)
            for v in range(2):
                store(GROUPS - 2 + v, v, 0)
            for v in range(2):
                sp.wait_ge(out_stored[v], 32 * (GROUPS // 2))

        @block.gpsimd
        def _(pool):
            def body(G, v, i):
                pool.wait_ge(od_ready, G + 1)
                pool.wait_ge(r_loaded[v], i * 32 + 32)
                nc.gpsimd.tensor_tensor(R[v][:], R[v][:], od[:], ALU.add).then_inc(out_ready, 1)

            groups(pool, body)

        @block.scalar
        def _(act):
            def body(G, v, i):
                act.wait_ge(turned, G + 1)
                wait(act, looked_up, G)
                nc.scalar.copy(ohTs[:], banks[0][0:NTILE, :]).then_inc(ohT_ready, 1)

            groups(act, body)

        @block.vector
        def _(dve):
            dve.wait_ge(ext_pe, 1)
            nc.vector.tensor_reduce(ext_T[:], banks[0][:, 0:P], AX.X, ALU.max)
            dve.drain()
            nc.vector.tensor_scalar(ext_diag[:], ident[:], ext_T[:], None, ALU.mult).then_inc(ext_step, 1)
            dve.wait_ge(ext_pe, 2)
            nc.vector.tensor_copy(ext[:].rearrange("p q i -> p (q i)"), banks[1][:, 0:P]).then_inc(ext_step, 1)
            dve.wait_ge(ext_step, 2)

            def body(G, v, i):
                dve.wait_ge(oq_loaded[v], i * 16 + 16)
                oh = oq[v][:, :, 0:NTILE]
                xs = oq[v][:, :, NTILE:NTILE + DS]
                for q in range(2):
                    nc.vector.tensor_tensor(prod[:, q, 0:N * NTILE].rearrange("p (t i) -> p t i", t=N), oh,
                                            ext[:, q, :].unsqueeze(1).to_broadcast([P, N, NTILE]), ALU.mult)
                dve.drain()
                for q in range(2):
                    nc.vector.tensor_reduce(e[:, q, :], prod[:, q, 0:N * NTILE].rearrange("p (t i) -> p t i", t=N),
                                            AX.X, ALU.add)
                dve.drain()
                nc.vector.tensor_tensor(rdn[:], e[:, 0, :], e[:, 1, :], ALU.add)
                nc.vector.tensor_tensor(v16[:], xs, e[:, 1, :].unsqueeze(2).to_broadcast([P, N, DS]), ALU.add)
                dve.drain()
                nc.vector.tensor_scalar_add(rdn[:], rdn[:], 1e-8)
                dve.drain()
                nc.vector.reciprocal(rdn[:], rdn[:])
                dve.drain()
                nc.vector.tensor_tensor(v16[:], v16[:], rdn[:].unsqueeze(2).to_broadcast([P, N, DS]), ALU.mult)
                dve.drain()
                nc.vector.tensor_scalar(v16[:], v16[:], 0.0, 1.0 - 1e-6, ALU.max, ALU.min)
                dve.drain()
                nc.vector.tensor_scalar(v16[:], v16[:], float(GRID), None, ALU.mult)
                dve.drain()
                nc.vector.tensor_copy(gi[:], v16[:])
                dve.drain()
                nc.vector.tensor_copy(gf[:], gi[:])
                dve.drain()
                nc.vector.tensor_tensor(gt[:], gf[:], v16[:], ALU.is_gt)
                dve.drain()
                nc.vector.tensor_tensor(gf[:], gf[:], gt[:], ALU.subtract)
                dve.drain()
                nc.vector.tensor_tensor(v16[:], v16[:], gf[:], ALU.subtract)
                cell = gf[:].rearrange("p t j -> p (t j)").unsqueeze(2).to_broadcast([P, N * DS, GRID])
                nc.vector.tensor_tensor(eq, cell, grid16[:].unsqueeze(1).to_broadcast([P, N * DS, GRID]), ALU.is_equal)
                dve.drain()
                dve.wait_ge(looked_up, G + 1)
                for q in range(2):
                    nc.vector.tensor_tensor(prod[:, q, :].rearrange("p (t g) -> p t g", g=GRID), eq,
                                            banks[1 + q][:].rearrange("p (t g) -> p t g", g=GRID), ALU.mult)
                dve.drain().then_inc(looked_taken, 1)
                for q, dst in ((0, bsel), (1, ssel)):
                    nc.vector.tensor_reduce(dst[:].rearrange("p t j -> p (t j)"),
                                            prod[:, q, :].rearrange("p (t g) -> p t g", g=GRID), AX.X, ALU.add)
                dve.drain()
                nc.vector.tensor_tensor(ssel[:], ssel[:], v16[:], ALU.mult)
                dve.drain()
                nc.vector.tensor_tensor(bsel[:], bsel[:], ssel[:], ALU.add)
                dve.drain()
                wait(dve, out_ready, G)
                nc.vector.tensor_tensor(od[:].rearrange("p t (i j) -> p t i j", j=DS),
                                        oh.unsqueeze(3).to_broadcast([P, N, NTILE, DS]),
                                        bsel[:].unsqueeze(2).to_broadcast([P, N, NTILE, DS]), ALU.mult
                                        ).then_inc(od_ready, 1)

            groups(dve, body)

        @block.tensor
        def _(pe):
            nc.tensor.transpose(banks[0][:, 0:P], acc[:].rearrange("p q i -> p (q i)"), ident[:]).then_inc(ext_pe, 1)
            pe.wait_ge(ext_step, 1)
            nc.tensor.matmul(banks[1][:, 0:P], ones[:], ext_diag[:], start=True, stop=True).then_inc(ext_pe, 1)
            pe.wait_ge(ext_step, 2)

            def body(G, v, i):
                pe.wait_ge(oq_loaded[v], i * 16 + 16)
                wait(pe, ohT_ready, G)
                pe.sem_inc(pe_steps3, 1)
                for t in range(N):
                    last_ = nc.tensor.transpose(banks[0][0:NTILE, t * P:(t + 1) * P], oq[v][:, t, 0:NTILE], ident[:])
                last_.then_inc(turned, 1)
                pe.wait_ge(ohT_ready, G + 1)
                wait(pe, looked_taken, G)
                for q in range(2):
                    for t in range(N):
                        last_ = nc.tensor.matmul(banks[1 + q][:, t * P:(t + 1) * P], ohTs[:, t * P:(t + 1) * P],
                                                 tab[:, q, :], start=True, stop=True)
                last_.then_inc(looked_up, 1)

            groups(pe, body)


def constants():
    f32 = np.float32
    H, D, C, T_ = 16, 32, 128, 4096
    start = 2.0 ** (-2.0 ** (-(np.log2(H) - 3)))
    slopes = np.array([start * start ** i for i in range(H)], f32)
    r = np.exp(-slopes).astype(f32).astype(np.float64)
    i = np.arange(C, dtype=np.float64)
    diff = i[None, :] - i[:, None]
    full = np.where(diff[None] >= 0, r[:, None, None] ** np.maximum(diff, 0)[None], 0.0)
    decay = full.reshape(4, 4, C, C).transpose(2, 1, 0, 3)
    q_dec = (r[:, None] ** (i[None, :] + 1)).reshape(4, 4, C)
    q_dec = np.repeat(q_dec.transpose(1, 0, 2), D, axis=0)
    k_dec = (r[:, None] ** (C - 1 - i[None, :])).T
    kv_mask = np.kron(np.eye(4), np.ones((D, D)))
    kv_dec = np.stack([kv_mask * np.repeat(r.reshape(4, 4)[g] ** float(C), D)[:, None] for g in range(4)], 1)
    freq = (f32(1.0 / 1024.0) ** np.linspace(0.0, 1.0, D // 4, dtype=f32)).astype(f32)
    theta = (np.arange(T_, dtype=f32)[:, None] * freq[None, :]).astype(f32)
    cos, sin = np.cos(theta.astype(np.float64)), np.sin(theta.astype(np.float64))
    rot = np.stack([np.concatenate([cos, cos], 1), np.concatenate([sin, -sin], 1)], 1)
    out = {
        "eye": np.eye(128), "decay": decay, "q_dec": q_dec, "k_dec": k_dec, "kv_dec": kv_dec,
        "kv_mask": np.broadcast_to(kv_mask[:, None], (128, 4, 128)), "rot": rot.reshape(T_ // 128, 128, 2, 16),
        "tie8": np.broadcast_to(7.0 - np.arange(8), (128, 8)),
        "tie64": np.broadcast_to(7.0 - np.arange(64) % 8, (128, 64)),
        "grid16": np.broadcast_to(np.arange(16.0), (128, 16)),
    }
    return {k: np.ascontiguousarray(v.astype(f32)) for k, v in out.items()}


def kernel(**inputs):
    import numpy as _np
    import concourse.bacc as _bacc
    from concourse import mybir as _mybir
    from concourse.bass_utils import run_bass_kernel_spmd as _run

    nc = _bacc.Bacc("TRN2", target_bir_lowering=False, num_devices=1)
    a = {k: _np.ascontiguousarray(v) for k, v in inputs.items()}
    const = constants()

    def per_group(v):
        return v.reshape(-1, 128, v[0].size).transpose(1, 0, 2)

    arrays = {
        "x": a["L0_attn_x"], "in_w": a["L0_attn_in_proj_w"], "xproj_w": a["L0_attn_x_proj_w"],
        "dt_w": a["L0_attn_dt_proj_w"], "out_w": a["L0_attn_out_proj_w"],
        "chan": _np.ascontiguousarray(_np.concatenate([
            per_group(a["L0_attn_conv_w"]), per_group(a["L0_attn_conv_b"]), per_group(a["L0_attn_D_param"]),
            per_group(a["L0_attn_dt_proj_b"]), per_group(a["L0_attn_A_log"])], axis=2)),
        "factors": a["L0_ffn_factors"], "bias": a["L0_ffn_bias"].reshape(1, -1),
        "Wq": a["L1_attn_Wq"], "Wk": a["L1_attn_Wk"], "Wv": a["L1_attn_Wv"], "Wo": a["L1_attn_Wo"],
        "rms_w": _np.ascontiguousarray(a["L1_attn_rms_w"].reshape(-1, 128).T),
        "gamma": a["L1_ffn_ln_gamma"].reshape(1, -1), "beta": a["L1_ffn_ln_beta"].reshape(1, -1),
        "bases": a["L1_ffn_spline_bases"], "slopes": a["L1_ffn_spline_slopes"],
        "oscale": a["L1_ffn_output_scale"].reshape(-1, 1),
        **const,
    }
    w = {k: nc.dram_tensor(f"in_{k}", v.shape, _mybir.dt.from_np(v.dtype), kind="ExternalInput").ap()
         for k, v in arrays.items()}
    shape = a["L0_attn_x"].shape
    x1 = nc.dram_tensor("x1", shape, F32, kind="Internal").ap()
    out = nc.dram_tensor("out_0", shape, F32, kind="ExternalOutput").ap()
    mamba_block(nc, w["x"], w["in_w"], w["chan"], w["xproj_w"], w["dt_w"], w["out_w"], w["eye"], x1)
    blocks_after(nc, x1, w, out)
    r = _run(nc, [{f"in_{k}": v for k, v in arrays.items()}], core_ids=[0])
    return r.results[0]["out_0"]
```

```python
import numpy as np
import concourse.bass as bass
from concourse import mybir
from contextlib import ExitStack

F32 = mybir.dt.float32
F32R = mybir.dt.float32r
BF16 = mybir.dt.bfloat16
I32 = mybir.dt.int32
ALU = mybir.AluOpType
ACT = mybir.ActivationFunctionType
AX = mybir.AxisListType

P = 128
T = 512
NT = T // P
LN_EPS = 1e-5
SSM_EPS = 1e-6
EXP_LN_SET = "natural_log_exp_and_others"


def wait(eng, sem, value):
    if not isinstance(value, int) or value > 0:
        eng.wait_ge(sem, value)


class Ring:

    def __init__(self, order, full, taken):
        self.order, self.full, self.taken = order, full, taken
        self.at = {use: q for q, (use, _) in enumerate(order)}
        self.per = {e: sum(1 for _, x in order if x == e) for e in taken}

    def bank(self, use):
        return self.at[use] % 2

    def filled(self, use, period):
        return period * len(self.order) + self.at[use] + 1

    def emptied(self, use, period):
        q = self.at[use]
        e = self.order[q][1]
        return self.taken[e], period * self.per[e] + sum(1 for _, x in self.order[:q + 1] if x == e)

    def before(self, use, period):
        q = self.at[use] - 2
        if q >= 0:
            return self.emptied(self.order[q][0], period)
        sem, value = self.emptied(self.order[q + len(self.order)][0], period)
        return sem, value - self.per[self.order[q + len(self.order)][1]]


def mamba_block(nc, x, in_w, chan, xproj_w, dt_w, out_w, eye, x1):
    BATCH, SEQ, HID = x.shape
    INTER = in_w.shape[1] // 2
    NSTATE = (xproj_w.shape[1] - dt_w.shape[0]) // 2
    RANK = dt_w.shape[0]
    KB = HID // P
    G = INTER // P
    GH = G // 2
    U = 2 * NSTATE
    SP_ = RANK + 2 * NSTATE
    NI = SEQ // T
    NCH = BATCH * NI
    SLOTS = 4
    assert BATCH == 2 and RANK == P and GH == 4 and NT == 4
    x_v = x.rearrange("b (i j p) d -> b i p j d", j=NT, p=P)
    x1_v = x1.rearrange("b (i j p) d -> b i j p d", j=NT, p=P)

    ctx = ExitStack()
    with ctx:
        def sb(name, shape, dt=F32):
            return ctx.enter_context(nc.sbuf_tensor(name, shape, dt))

        def ps(name, shape):
            return ctx.enter_context(nc.psum_tensor(name, shape, F32))

        def sem(name):
            return ctx.enter_context(nc.semaphore(name))

        w_in = sb("w_in", [P, KB, 2 * INTER])
        w_xp = sb("w_xp", [P, G, SP_])
        w_dt = sb("w_dt", [P, INTER])
        w_out = sb("w_out", [P, G, HID])
        ch = sb("ch", [P, G, 7 + NSTATE])
        ident = sb("ident", [P, P])
        minus_half = sb("minus_half", [P, NT * 3])
        xt = sb("xt", [P, NT, HID])
        xnT = sb("xnT", [P, KB, T])
        hid = [sb(f"hid{i}", [P, T + 3]) for i in range(2)]
        hist = sb("hist", [P, BATCH, G, 3])
        u = [sb(f"u{i}", [P, G, T]) for i in range(2)]
        gate = sb("gate", [P, G, T])
        dt = [sb(f"dt{i}", [P, GH, T]) for i in range(2)]
        dtu = sb("dtu", [P, GH, T])
        s = [sb(f"s{i}", [P, GH, T]) for i in range(SLOTS)]
        Bb = [sb(f"Bb{i}", [P, T]) for i in range(2)]
        Cb = [sb(f"Cb{i}", [P, T]) for i in range(2)]
        state = sb("state", [P, BATCH, U, GH])
        res = [sb(f"res{i}", [P, HID]) for i in range(2)]
        ssm = sb("ssm", [P, NT, SP_])
        ssm_sq = sb("ssm_sq", [P, NT, SP_])
        dtnT = sb("dtnT", [P, T])
        bcT = sb("bcT", [2 * NSTATE, T])
        st6 = sb("st6", [P, NT, 6])
        mv = sb("mv", [P, NT, 2])
        ve = sb("ve", [P, NT])
        rstd = sb("rstd", [P, NT])
        ssq = sb("ssq", [P, NT, 3])
        rssm = sb("rssm", [P, NT, 3])

        Y = [ps(f"Y{g}", [P, T]) for g in range(GH)]
        DA = [ps(f"DA{i}", [P, T]) for i in range(2)]
        PJ = [ps(f"PJ{i}", [P, T]) for i in range(2)]
        bc = [nc.dram_tensor(f"bc{i}", (2 * NSTATE, T), F32, kind="Internal").ap() for i in range(2)]

        w_loaded, x_loaded = sem("w_loaded"), sem("x_loaded")
        w_hid_loaded, small_loaded = sem("w_hid_loaded"), sem("small_loaded")
        consts_ready = sem("consts_ready")
        stats_ready, rstd_ready, xn_ready = sem("stats_ready"), sem("rstd_ready"), sem("xn_ready")
        conv_done, u_ready, gate_ready = sem("conv_done"), sem("u_ready"), sem("gate_ready")
        sq_ready, ssq_ready, rssm_ready, ssm_ready = (
            sem("sq_ready"), sem("ssq_ready"), sem("rssm_ready"), sem("ssm_ready"))
        dt_min, dt_log, dt_ready, dtu_ready = sem("dt_min"), sem("dt_log"), sem("dt_ready"), sem("dtu_ready")
        bc_stored, sp_steps = sem("bc_stored"), sem("sp_steps")
        b_loaded = [sem(f"b_loaded{i}") for i in range(2)]
        c_loaded = [sem(f"c_loaded{i}") for i in range(2)]
        dbu_ready, da_ready, scan_done, state_saved = (
            sem("dbu_ready"), sem("da_ready"), sem("scan_done"), sem("state_saved"))
        z_ready, sum_done, y_taken, y_ready = sem("z_ready"), sem("sum_done"), sem("y_taken"), sem("y_ready")
        res_loaded = [sem(f"res_loaded{i}") for i in range(2)]
        x1_ready = sem("x1_ready")
        x1_stored = [sem(f"x1_stored{i}") for i in range(2)]

        def ring(order, tag):
            return Ring(order, sem(f"proj_full_{tag}"),
                        {"act": sem(f"proj_taken_act_{tag}"), "dve": sem(f"proj_taken_dve_{tag}")})

        def uses(name, n, e):
            return [((name, j), e) for j in range(n)]

        ahead = ring(uses("xT", KB, "act") + uses("hid", G, "act") + uses("xp", 2, "act")
                     + uses("turn", 2, "act") + uses("dt0", GH, "act") + uses("gate", GH, "act"), "ahead")
        steady = ring(uses("gate", G, "act")[GH:] + uses("xT", KB, "act") + uses("out", NT, "dve")
                      + uses("dt1", GH, "act") + uses("hid", G, "act") + uses("xp", 2, "act")
                      + uses("gate", 2, "act") + uses("turn", 2, "act") + [(("gate", 2), "act")]
                      + uses("dt0", GH, "act") + [(("gate", 3), "act")], "steady")
        after = ring(uses("out", NT, "dve"), "after")

        BLOCKS = {}
        BLOCKS.update({m: ("gate", GH + m, None) for m in range(GH)})
        BLOCKS.update({4 + 2 * j + part: ("out", j, part) for j in range(NT) for part in range(2)})
        BLOCKS.update({13 + m: ("hid", m, None) for m in range(G)})
        BLOCKS.update({24: ("gate", 0, None), 25: ("gate", 1, None), 26: ("gate", 2, None), 28: ("gate", 3, None)})
        UNIT_OF = {b: k for k, b in BLOCKS.items()}
        K_DT1, K_XT, K_SILU, K_XP, K_TURN, K_DT0 = 12, 4, 21, (22, 23), 26, 27

        def blocks(k):
            return [BLOCKS[k]] if k in BLOCKS else []

        block = ctx.enter_context(nc.Block())

        def periods(eng, body):
            for b in range(BATCH):
                body(0, b, b, b == 0, False)
            with eng.Fori(1, NI - 1) as i:
                for b in range(BATCH):
                    body(i, b, i * BATCH + b, False, False)
            for b in range(BATCH):
                body(NI - 1, b, (NI - 1) * BATCH + b, False, b == BATCH - 1)

        @block.sync
        def _(sp):
            def held(sem_, value):
                wait(sp, sem_, value)
                sp.sem_inc(sp_steps, 1)

            for cols, loaded in ((slice(0, INTER), w_hid_loaded), (slice(INTER, 2 * INTER), w_loaded)):
                for m in range(KB):
                    sp.dma_start(w_in[:, m, cols], in_w[m * P:(m + 1) * P, cols]).then_inc(loaded, 16)
            sp.dma_start(w_xp[:], xproj_w.rearrange("(g p) n -> p g n", p=P)).then_inc(w_loaded, 16)
            sp.dma_start(w_dt[:], dt_w).then_inc(w_loaded, 16)
            sp.dma_start(w_out[:], out_w.rearrange("(g p) n -> p g n", p=P)).then_inc(w_loaded, 16)

            def load_b(c, k, slot):
                held(dbu_ready, c * U + (k - 1))
                sp.dma_start(Bb[k % 2][:], bc[slot][k % NSTATE:k % NSTATE + 1, :].to_broadcast([P, T])
                             ).then_inc(b_loaded[k % 2], 16)

            def load_c(c, k, slot):
                held(z_ready, c * U + (k - 1))
                sp.dma_start(Cb[k % 2][:], bc[slot][NSTATE + k % NSTATE:NSTATE + k % NSTATE + 1, :]
                             .to_broadcast([P, T])).then_inc(c_loaded[k % 2], 16)

            def store_bc(ring_, period, c_next, slot):
                s_, v = ring_.emptied(("turn", 1), period)
                held(s_, v)
                sp.dma_start(bc[slot], bcT[:]).then_inc(bc_stored, 16)

            store_bc(ahead, 0, 0, 0)
            sp.wait_ge(bc_stored, 16)
            for k in range(2):
                load_b(0, k, 0)
                load_c(0, k, 0)

            def load_res(i_prev, b_prev, c_prev, j):
                held(x1_stored[j % 2], 16 * (c_prev * 2 + j // 2))
                sp.dma_start(res[j % 2][:], x_v[b_prev, i_prev, :, j, :]).then_inc(res_loaded[j % 2], 16)

            def store_x1(i_prev, b_prev, c_prev, j):
                held(x1_ready, c_prev * NT + j + 1)
                sp.dma_start(x1_v[b_prev, i_prev, j], res[j % 2][:]).then_inc(x1_stored[j % 2], 16)

            def body(i, b, c, first, last):
                i_prev, b_prev, c_prev = (i, 0, c - 1) if b else (i - 1, 1, c - 1)
                i_next, b_next = (i + 1, 0) if b else (i, 1)
                for k in range(U):
                    if k == 0 and not last:
                        held(dt_ready, c * 2 + 1)
                        sp.dma_start(xt[:], x_v[b_next, i_next]).then_inc(x_loaded, 16)
                    if not first:
                        if k in (1, 2):
                            load_res(i_prev, b_prev, c_prev, k - 1)
                        for j in range(NT):
                            if k == UNIT_OF[("out", j, 1)] + 3:
                                store_x1(i_prev, b_prev, c_prev, j)
                        for j in range(2, NT):
                            if k == UNIT_OF[("out", j - 2, 1)] + 4:
                                load_res(i_prev, b_prev, c_prev, j)
                    if k == 28 and not last:
                        store_bc(steady, c, c + 1, 1 - b)
                    if k + 2 < U:
                        load_b(c, k + 2, b)
                        load_c(c, k + 2, b)
                    elif not last:
                        if k + 2 == U:
                            held(bc_stored, 16 * (c + 2))
                        held(dbu_ready, c * U + k + 1)
                        n = k + 2 - U
                        sp.dma_start(Bb[n % 2][:], bc[1 - b][n:n + 1, :].to_broadcast([P, T])
                                     ).then_inc(b_loaded[n % 2], 16)
                        held(z_ready, c * U + k + 1)
                        sp.dma_start(Cb[n % 2][:], bc[1 - b][NSTATE + n:NSTATE + n + 1, :]
                                     .to_broadcast([P, T])).then_inc(c_loaded[n % 2], 16)

            periods(sp, body)
            for j in range(NT):
                load_res(NI - 1, 1, NCH - 1, j)
                store_x1(NI - 1, 1, NCH - 1, j)
            for j in range(2):
                sp.wait_ge(x1_stored[j], 16 * 2 * NCH)

        @block.gpsimd
        def _(pool):
            nc.gpsimd.memset(minus_half[:], -0.5)
            nc.gpsimd.memset(state[:], 0.0)
            nc.gpsimd.memset(hist[:], 0.0)
            pool.drain().then_inc(consts_ready, 1)

            def ln_power(c_next):
                wait(pool, stats_ready, c_next + 1)
                nc.gpsimd.tensor_tensor(rstd[:], ve[:], minus_half[:, 0:NT], ALU.pow).then_inc(rstd_ready, 1)

            def ssm_power(c_next):
                wait(pool, ssq_ready, c_next + 1)
                nc.gpsimd.tensor_tensor(rssm[:].rearrange("p j n -> p (j n)"), ssq[:].rearrange("p j n -> p (j n)"),
                                        minus_half[:], ALU.pow).then_inc(rssm_ready, 1)

            ln_power(0)
            ssm_power(0)

            def body(i, b, c, first, last):
                for k in range(U):
                    h = k // NSTATE
                    if k == 3 and not last:
                        ln_power(c + 1)
                    if k == 26 and not last:
                        ssm_power(c + 1)
                    if k % NSTATE == 0:
                        wait(pool, dt_ready, 2 * c + h + 1)
                        wait(pool, dbu_ready, c * U + k)
                        nc.gpsimd.tensor_tensor(dtu[:], dt[h][:], u[b][:, GH * h:GH * h + GH, :], ALU.mult
                                                ).then_inc(dtu_ready, 1)
                        wait(pool, dtu_ready, 2 * c + h + 1)
                    wait(pool, b_loaded[k % 2], 16 * (c * (U // 2) + k // 2 + 1))
                    wait(pool, sum_done, c * U + k + 1 - SLOTS)
                    nc.gpsimd.tensor_tensor(s[k % SLOTS][:], dtu[:], Bb[k % 2][:].unsqueeze(1).to_broadcast([P, GH, T]),
                                            ALU.mult).then_inc(dbu_ready, 1)

            periods(pool, body)

        @block.scalar
        def _(act):
            act.dma_start(xt[:], x_v[0, 0]).then_inc(x_loaded, 16)
            act.dma_start(ch[:], chan).then_inc(small_loaded, 16)
            act.dma_start(ident[:], eye).then_inc(small_loaded, 16)
            act.wait_ge(small_loaded, 32)
            nc.scalar.preload_act_table_set(EXP_LN_SET)
            nc.scalar.activation(ch[:, :, 7:], ch[:, :, 7:], ACT.Exp)
            act.drain()
            nc.scalar.mul(ch[:, :, 7:], ch[:, :, 7:], -1.0)
            act.drain().then_inc(consts_ready, 1)

            def take(ring_, use, period, out, part=P):
                act.wait_ge(ring_.full, ring_.filled(use, period))
                nc.scalar.copy(out, PJ[ring_.bank(use)][0:part, :]).then_inc(ring_.taken["act"], 1)

            def take_hid(ring_, m, period, c_next, slot):
                wait(act, conv_done, c_next * G + m - 1)
                act.wait_ge(ring_.full, ring_.filled(("hid", m), period))
                bank = PJ[ring_.bank(("hid", m))]
                nc.scalar.activation(u[slot][:, m, :], bank[:], ACT.Identity, bias=ch[:, m, 4:5], scale=ch[:, m, 3:4])
                nc.scalar.copy(hid[m % 2][:, 3:T + 3], bank[:]).then_inc(ring_.taken["act"], 1)

            def silu_u(c_next, slot, h):
                act.wait_ge(conv_done, c_next * G + (h + 1) * GH)
                part = u[slot][:, GH * h:GH * h + GH, :]
                nc.scalar.activation(part, part, ACT.Silu).then_inc(u_ready, 1)

            def square(ring_, n, period):
                act.wait_ge(ring_.full, ring_.filled(("xp", n), period))
                bank = PJ[ring_.bank(("xp", n))][:, 0:2 * SP_].rearrange("p (j n) -> p j n", j=2)
                nc.scalar.activation(ssm_sq[:, 2 * n:2 * n + 2, :], bank, ACT.Square).then_inc(sq_ready, 1)
                nc.scalar.copy(ssm[:, 2 * n:2 * n + 2, :], bank).then_inc(ring_.taken["act"], 1)

            def turned(ring_, period, c_next):
                take(ring_, ("turn", 0), period, dtnT[:])
                wait(act, bc_stored, 16 * c_next)
                take(ring_, ("turn", 1), period, bcT[:], 2 * NSTATE)

            def dt_bias(ring_, h, g, period):
                use = (f"dt{h}", g)
                act.wait_ge(ring_.full, ring_.filled(use, period))
                nc.scalar.activation(dt[h][:, g, :], PJ[ring_.bank(use)][:], ACT.Identity,
                                     bias=ch[:, GH * h + g, 6:7]).then_inc(ring_.taken["act"], 1)

            def dt_exp(n):
                act.wait_ge(dt_min, n + 1)
                nc.scalar.activation(xt[:], xt[:], ACT.Exp)

            def dt_log_():
                act.drain()
                nc.scalar.activation(xt[:], xt[:], ACT.Ln, bias=1.0).then_inc(dt_log, 1)

            for kb in range(KB):
                take(ahead, ("xT", kb), 0, xnT[:, kb, :])
            for m in range(G):
                take_hid(ahead, m, 0, 0, 0)
            for h in range(2):
                silu_u(0, 0, h)
            for n in range(2):
                square(ahead, n, 0)
            nc.scalar.preload_act_table_set(EXP_LN_SET)
            turned(ahead, 0, 0)
            for g in range(GH):
                dt_bias(ahead, 0, g, 0)
            for m in range(GH):
                take(ahead, ("gate", m), 0, gate[:, m, :])
            dt_exp(0)
            dt_log_()

            def body(i, b, c, first, last):
                nc.scalar.preload_act_table_set(EXP_LN_SET)

                def piece(k):
                    if k == K_TURN and not last:
                        turned(steady, c, c + 1)
                    for kind, m, _ in blocks(k):
                        if kind == "gate" and not (last and m < GH):
                            wait(act, y_ready, 2 * c + (1 if m < GH else 0))
                            take(steady, ("gate", m), c, gate[:, m, :])
                        if kind == "hid" and not last:
                            take_hid(steady, m, c, c + 1, 1 - b)
                    if k == K_XT:
                        if last:
                            act.drain().then_inc(steady.taken["act"], KB)
                        else:
                            for kb in range(KB):
                                take(steady, ("xT", kb), c, xnT[:, kb, :])
                    if k == K_DT1:
                        for g in range(GH):
                            dt_bias(steady, 1, g, c)
                    if last:
                        return
                    if k in K_XP:
                        square(steady, k - K_XP[0], c)
                    if k == K_DT0:
                        for g in range(GH):
                            dt_bias(steady, 0, g, c)

                def long_piece(k):
                    if k in (6, 9):
                        half = slice(0, GH) if k == 6 else slice(GH, G)
                        nc.scalar.activation(gate[:, half, :], gate[:, half, :], ACT.Silu).then_inc(gate_ready, 1)
                        nc.scalar.preload_act_table_set(EXP_LN_SET)
                    if k == 13:
                        dt_exp(2 * c + 1)
                        dt_log_()
                    if k in (K_SILU - 3, K_SILU) and not last:
                        silu_u(c + 1, 1 - b, 0 if k < K_SILU else 1)
                        nc.scalar.preload_act_table_set(EXP_LN_SET)
                    if k == 28 and not last:
                        dt_exp(2 * c + 2)
                        dt_log_()

                for k in range(U):
                    h, n = k // NSTATE, k % NSTATE
                    for g in range(GH):
                        if n == 0 and g == 0:
                            wait(act, dt_ready, 2 * c + h + 1)
                        wait(act, scan_done, GH * (c * U + k) + g - 1)
                        nc.scalar.activation(DA[g % 2][:], dt[h][:, g, :], ACT.Exp,
                                             scale=ch[:, GH * h + g, 7 + n:8 + n]).then_inc(da_ready, 1)
                        if g == 1:
                            piece(k - 1)
                    long_piece(k - 1)

            periods(act, body)

        @block.vector
        def _(dve):
            def ln_stats(c_next):
                wait(dve, x_loaded, 16 * (c_next + 1))
                for j in range(NT):
                    nc.vector.bn_stats(st6[:, j, :], xt[:, j, :])
                dve.drain()
                for j in range(NT):
                    nc.vector.bn_aggr(mv[:, j, :], st6[:, j, :])
                dve.drain()
                nc.vector.tensor_scalar(ve[:], mv[:, :, 1], 1.0, LN_EPS, ALU.mult, ALU.add).then_inc(stats_ready, 1)

            def ln_apply(c_next):
                wait(dve, rstd_ready, c_next + 1)
                for j in range(NT):
                    last_ = nc.vector.tensor_scalar(xt[:, j, :], xt[:, j, :], mv[:, j, 0:1], rstd[:, j:j + 1],
                                                    ALU.subtract, ALU.mult)
                last_.then_inc(xn_ready, 1)

            def conv(ring_, m, period, b_next, slot):
                out = u[slot][:, m, :]
                h_ = hid[m % 2]
                nc.vector.tensor_copy(h_[:, 0:3], hist[:, b_next, m, :])
                s_, v = ring_.emptied(("hid", m), period)
                dve.drain()
                dve.wait_ge(s_, v)
                nc.vector.tensor_copy(hist[:, b_next, m, :], h_[:, T:T + 3])
                for tap in range(3):
                    if tap > 0:
                        dve.drain()
                    last_ = nc.vector.scalar_tensor_tensor(out, h_[:, tap:tap + T], ch[:, m, tap:tap + 1], out,
                                                           ALU.mult, ALU.add)
                last_.then_inc(conv_done, 1)

            def ssm_sums(c_next):
                wait(dve, sq_ready, 2 * (c_next + 1))
                nc.vector.tensor_reduce(ssq[:, :, 0], ssm_sq[:, :, 0:RANK], AX.X, ALU.add)
                nc.vector.tensor_reduce(ssq[:, :, 1:3], ssm_sq[:, :, RANK:].rearrange("p j (q n) -> p j q n", q=2),
                                        AX.X, ALU.add)
                dve.drain()
                nc.vector.tensor_scalar(ssq[:, :, 0], ssq[:, :, 0], 1.0 / RANK, SSM_EPS, ALU.mult, ALU.add)
                nc.vector.tensor_scalar(ssq[:, :, 1:3], ssq[:, :, 1:3], 1.0 / NSTATE, SSM_EPS, ALU.mult, ALU.add)
                dve.drain().then_inc(ssq_ready, 1)

            def ssm_norm(ring_, period, c_next):
                wait(dve, rssm_ready, c_next + 1)
                s_, v = ring_.emptied(("xp", 1), period)
                dve.wait_ge(s_, v)
                nc.vector.tensor_tensor(ssm[:, :, 0:RANK], ssm[:, :, 0:RANK],
                                        rssm[:, :, 0:1].to_broadcast([P, NT, RANK]), ALU.mult)
                for q in range(2):
                    lo = RANK + q * NSTATE
                    last_ = nc.vector.tensor_tensor(ssm[:, :, lo:lo + NSTATE], ssm[:, :, lo:lo + NSTATE],
                                                    rssm[:, :, 1 + q:2 + q].to_broadcast([P, NT, NSTATE]), ALU.mult)
                last_.then_inc(ssm_ready, 1)

            def dt_floor(ring_, h, period):
                s_, v = ring_.emptied((f"dt{h}", GH - 1), period)
                dve.wait_ge(s_, v)
                nc.vector.tensor_scalar_min(xt[:], dt[h][:], 30.0).then_inc(dt_min, 1)

            def dt_max(h, n):
                dve.wait_ge(dt_log, n + 1)
                nc.vector.tensor_tensor(dt[h][:], dt[h][:], xt[:], ALU.max).then_inc(dt_ready, 1)

            def add_res(ring_, j, period, c_prev):
                dve.wait_ge(ring_.full, ring_.filled(("out", j), period))
                wait(dve, res_loaded[j % 2], 16 * (c_prev * 2 + j // 2 + 1))
                nc.vector.tensor_tensor(res[j % 2][:], PJ[ring_.bank(("out", j))][:], res[j % 2][:], ALU.add
                                        ).then_inc(x1_ready, 1)
                dve.wait_ge(x1_ready, c_prev * NT + j + 1)
                dve.sem_inc(ring_.taken["dve"], 1)

            def y_half(h, c, slot):
                dve.wait_ge(sum_done, c * U + NSTATE * (h + 1))
                for g in range(GH):
                    nc.vector.scalar_tensor_tensor(u[slot][:, GH * h + g, :], u[slot][:, GH * h + g, :],
                                                   ch[:, GH * h + g, 5:6], Y[g][:], ALU.mult, ALU.add
                                                   ).then_inc(y_taken, 1)

            def y_gate(h, c, slot):
                wait(dve, gate_ready, 2 * c + h + 1)
                dve.wait_ge(y_taken, (2 * c + h + 1) * GH)
                part = slice(GH * h, GH * h + GH)
                nc.vector.tensor_tensor(u[slot][:, part, :], u[slot][:, part, :], gate[:, part, :], ALU.mult
                                        ).then_inc(y_ready, 1)

            dve.wait_ge(consts_ready, 2)
            ln_stats(0)
            ln_apply(0)
            for m in range(G):
                conv(ahead, m, 0, 0, 0)
            ssm_sums(0)
            ssm_norm(ahead, 0, 0)
            dt_floor(ahead, 0, 0)
            dt_max(0, 0)

            def body(i, b, c, first, last):
                def piece(k):
                    if k == 1 and not last:
                        ln_stats(c + 1)
                    if k == 3 and not last:
                        ln_apply(c + 1)
                    if k == 13:
                        dt_floor(steady, 1, c)
                    if k == 14:
                        dt_max(1, 2 * c + 1)
                    for j in range(NT):
                        if UNIT_OF[("out", j, 1)] + 1 == k:
                            if first:
                                dve.drain().then_inc(steady.taken["dve"], 1)
                            else:
                                add_res(steady, j, c, c - 1)
                    if not last:
                        for kind, m, _ in blocks(k - 1):
                            if kind == "hid":
                                conv(steady, m, c, 1 - b, 1 - b)
                        if k == 24:
                            ssm_sums(c + 1)
                        if k == 25:
                            ssm_norm(steady, c, c + 1)
                        if k == 28:
                            dt_floor(steady, 0, c)
                        if k == 29:
                            dt_max(0, 2 * c + 2)
                    if k == 0 and not first:
                        y_half(1, c - 1, 1 - b)
                        y_gate(1, c - 1, 1 - b)
                    if k == NSTATE:
                        y_half(0, c, b)
                    if k == 22:
                        y_gate(0, c, b)

                for k in range(U):
                    wait(dve, dbu_ready, c * U + k + 1)
                    for g in range(GH):
                        wait(dve, da_ready, GH * (c * U + k) + g + 1)
                        nc.vector.tensor_tensor_scan(s[k % SLOTS][:, g, :], DA[g % 2][:], s[k % SLOTS][:, g, :],
                                                     state[:, b, k, g:g + 1], ALU.mult, ALU.add
                                                     ).then_inc(scan_done, 1)
                    wait(dve, scan_done, GH * (c * U + k + 1))
                    nc.vector.tensor_copy(state[:, b, k, :], s[k % SLOTS][:, :, T - 1]).then_inc(state_saved, 1)
                    wait(dve, c_loaded[k % 2], 16 * (c * (U // 2) + k // 2 + 1))
                    wait(dve, state_saved, c * U + k + 1)
                    nc.vector.tensor_tensor(s[k % SLOTS][:], s[k % SLOTS][:], Cb[k % 2][:].unsqueeze(1).to_broadcast([P, GH, T]),
                                            ALU.mult).then_inc(z_ready, 1)
                    piece(k)

            periods(dve, body)
            y_half(1, NCH - 1, 1)
            y_gate(1, NCH - 1, 1)
            for j in range(NT):
                add_res(after, j, 0, NCH - 1)

        @block.tensor
        def _(pe):
            def bank_of(ring_, use, period):
                sem_, value = ring_.before(use, period)
                wait(pe, sem_, value)
                return PJ[ring_.bank(use)]

            def turn_x(ring_, period, c_next):
                wait(pe, xn_ready, c_next + 1)
                for kb in range(KB):
                    bank = bank_of(ring_, ("xT", kb), period)
                    for j in range(NT):
                        last_ = nc.tensor.transpose(bank[:, j * P:(j + 1) * P], xt[:, j, kb * P:(kb + 1) * P], ident[:])
                    last_.then_inc(ring_.full, 1)

            def project(ring_, use, period, lo):
                bank = bank_of(ring_, use, period)
                for kb in range(KB):
                    last_ = nc.tensor.matmul(bank[:], w_in[:, kb, lo:lo + P], xnT[:, kb, :],
                                             start=(kb == 0), stop=(kb == KB - 1))
                last_.then_inc(ring_.full, 1)

            def x_proj(ring_, n, period, c_next, slot):
                wait(pe, u_ready, 2 * (c_next + 1))
                bank = bank_of(ring_, ("xp", n), period)
                for j in range(2):
                    for g in range(G):
                        t0 = (2 * n + j) * P
                        last_ = nc.tensor.matmul(bank[:, j * SP_:(j + 1) * SP_], u[slot][:, g, t0:t0 + P],
                                                 w_xp[:, g, :], start=(g == 0), stop=(g == G - 1))
                last_.then_inc(ring_.full, 1)

            def turn_ssm(ring_, period, c_next):
                wait(pe, ssm_ready, c_next + 1)
                bank = bank_of(ring_, ("turn", 0), period)
                for j in range(NT):
                    last_ = nc.tensor.transpose(bank[:, j * P:(j + 1) * P], ssm[:, j, 0:RANK], ident[:])
                last_.then_inc(ring_.full, 1)
                bank = bank_of(ring_, ("turn", 1), period)
                for j in range(NT):
                    last_ = nc.tensor.transpose(bank[0:2 * NSTATE, j * P:(j + 1) * P], ssm[:, j, RANK:], ident[:])
                last_.then_inc(ring_.full, 1)

            def dt_proj(ring_, h, g, period):
                sem_, value = ring_.emptied(("turn", 0), period)
                if h == 0:
                    pe.wait_ge(sem_, value)
                bank = bank_of(ring_, (f"dt{h}", g), period)
                lo = (GH * h + g) * P
                nc.tensor.matmul(bank[:], w_dt[:, lo:lo + P], dtnT[:], start=True, stop=True).then_inc(ring_.full, 1)

            def out_proj(ring_, j, part, period, slot):
                bank = bank_of(ring_, ("out", j), period) if part == 0 else PJ[ring_.bank(("out", j))]
                for g in range(GH * part, GH * part + GH):
                    last_ = nc.tensor.matmul(bank[:], u[slot][:, g, j * P:(j + 1) * P], w_out[:, g, :],
                                             start=(g == 0), stop=(g == G - 1))
                if part == 1:
                    last_.then_inc(ring_.full, 1)

            pe.wait_ge(small_loaded, 32)
            turn_x(ahead, 0, 0)
            pe.wait_ge(ahead.taken["act"], KB)
            pe.wait_ge(w_hid_loaded, 16 * KB)
            for m in range(G):
                project(ahead, ("hid", m), 0, m * P)
            pe.wait_ge(w_loaded, 16 * (KB + 3))
            for n in range(2):
                x_proj(ahead, n, 0, 0, 0)
            turn_ssm(ahead, 0, 0)
            for g in range(GH):
                dt_proj(ahead, 0, g, 0)
            for m in range(GH):
                project(ahead, ("gate", m), 0, INTER + m * P)
            pe.wait_ge(ahead.taken["act"], ahead.per["act"])

            def body(i, b, c, first, last):
                def pieces(k):
                    if k == K_XT:
                        if last:
                            pe.drain().then_inc(steady.full, KB)
                        else:
                            turn_x(steady, c, c + 1)
                    if k == K_TURN and not last:
                        turn_ssm(steady, c, c + 1)
                    for kind, m, part in blocks(k):
                        if kind == "gate" and not (last and m < GH):
                            project(steady, ("gate", m), c, INTER + m * P)
                        if kind == "out":
                            if first:
                                if part == 0:
                                    pe.drain().then_inc(steady.full, 1)
                            else:
                                if m == 0 and part == 0:
                                    pe.wait_ge(y_ready, 2 * c)
                                out_proj(steady, m, part, c, 1 - b)
                        if kind == "hid" and not last:
                            if m == 0:
                                pe.wait_ge(*steady.emptied(("xT", KB - 1), c))
                            project(steady, ("hid", m), c, m * P)
                    if k == K_DT1:
                        for g in range(GH):
                            dt_proj(steady, 1, g, c)
                    if last:
                        return
                    if k in K_XP:
                        x_proj(steady, k - K_XP[0], c, c + 1, 1 - b)
                    if k == K_DT0:
                        for g in range(GH):
                            dt_proj(steady, 0, g, c)

                for k in range(U):
                    pieces(k)
                    h, n = k // NSTATE, k % NSTATE
                    if n == 0:
                        wait(pe, y_taken, (2 * c + h) * GH)
                    pe.wait_ge(z_ready, c * U + k + 1)
                    for g in range(GH):
                        last_ = nc.tensor.matmul(Y[g][:], ident[:], s[k % SLOTS][:, g, :],
                                                 start=(n == 0), stop=(n == NSTATE - 1))
                    last_.then_inc(sum_done, 1)

            periods(pe, body)
            pe.wait_ge(y_ready, 2 * NCH)
            for j in range(NT):
                for part in range(2):
                    if part == 0 and j >= 2:
                        pe.wait_ge(after.taken["dve"], j - 1)
                    bank = PJ[after.bank(("out", j))]
                    for g in range(GH * part, GH * part + GH):
                        last_ = nc.tensor.matmul(bank[:], u[1][:, g, j * P:(j + 1) * P], w_out[:, g, :],
                                                 start=(g == 0), stop=(g == G - 1))
                last_.then_inc(after.full, 1)



def blocks_after(nc, x1, w, out):
    BATCH, SEQ, HID = x1.shape
    KB = HID // P
    RANKS = w["factors"].shape[0]
    TILES = BATCH * SEQ // P
    HEADS, HD = 16, 32
    HG = HEADS * HD // P
    ROT = 8
    NTILE, DS, GRID = w["slopes"].shape
    NCL = NTILE // 8
    BIG = 1e30
    RMS_EPS = 1e-5
    x1_v = x1.rearrange("b (i p) d -> b i p d", p=P)
    out_v = out.rearrange("b (i p) d -> b i p d", p=P)
    LAST_STAGE = 6

    ctx = ExitStack()
    with ctx:
        def sb(name, shape, dt=F32):
            return ctx.enter_context(nc.sbuf_tensor(name, shape, dt))

        def sem(name):
            return ctx.enter_context(nc.semaphore(name))

        w_high, w_low = ({n: sb(f"w_{part}_{n}", [P, KB, HID], F32R) for n in ("f", "q", "k", "v", "o")}
                         for part in ("high", "low"))
        rms_w = sb("rms_w", [P, KB])
        ident = sb("ident2", [P, P])
        ones = sb("ones", [P, P])
        decay = sb("decay", [P, 4, HG, P])
        q_dec = sb("q_dec", [P, HG, P])
        k_dec = sb("k_dec", [P, HEADS])
        kv_dec = sb("kv_dec", [P, HG, P])
        kv_mask = sb("kv_mask", [P, HG, P])
        bias_b = sb("bias_b", [P, HID])
        gamma_b = sb("gamma_b", [P, HID])
        beta_b = sb("beta_b", [P, HID])
        sign_b = sb("sign_b", [P, HID], BF16)
        tie8 = sb("tie8", [P, 8])
        tie64 = sb("tie64", [P, NTILE])
        grid16 = sb("grid16", [P, GRID])
        tab = sb("tab", [NTILE, 2, DS * GRID])
        oscale = sb("oscale", [NTILE, 1])
        smean = sb("smean", [NTILE, DS])

        x1t = [sb(f"x1t{i}", [P, HID]) for i in range(2)]
        rot = [sb(f"rot{i}", [P, 2, 2 * ROT]) for i in range(2)]
        xa = [sb(f"xa{i}", [P, HID]) for i in range(2)]
        xaT = [sb(f"xaT{i}", [P, KB, P], F32R) for i in range(2)]
        x2_all = sb("x2_all", [P, 4, HID])
        x2 = [x2_all[:, i, :] for i in range(4)]
        xb = [sb(f"xb{i}", [P, HID]) for i in range(2)]
        xbT = [sb(f"xbT{i}", [P, KB, P], F32R) for i in range(2)]
        qk_all = sb("qk_all", [P, 4, HID])
        qk = [qk_all[:, 2 * i:2 * i + 2, :] for i in range(2)]
        rc = sb("rc", [P, 2 * HEADS, 2, ROT])
        rs_ = sb("rs", [P, 2 * HEADS, 2, ROT])
        vv = [sb(f"vv{i}", [P, HID]) for i in range(2)]
        kd = [sb(f"kd{i}", [P, HID]) for i in range(2)]
        qTs = sb("qTs", [P, HG, P])
        qdT = sb("qdT", [P, HG, P])
        kTs = sb("kTs", [P, HG, P])
        scm = sb("scm", [P, 4, HG, P])
        w_part = [x2_all[:], scm[:].rearrange("p r g n -> p r (g n)")]
        w_sum = qk_all[:]
        kv = [sb(f"kv{i}", [P, HG, P]) for i in range(BATCH)]
        kvd = sb("kvd", [P, HG, P])
        kvu = sb("kvu", [P, HG, P])
        at_s = [sb(f"at_s{i}", [P, HID]) for i in range(2)]
        junk = sb("junk", [P, HID])
        sdiag = junk[0:NTILE, :].rearrange("a (i j) -> a i j", j=DS)
        rsum = [sb(f"rsum{i}", [P, 1]) for i in range(2)]
        rrms = [sb(f"rrms{i}", [P, 1]) for i in range(2)]
        aTs = [sb(f"aTs{i}", [P, KB, P], F32R) for i in range(2)]
        x3 = [sb(f"x3_{i}", [P, HID]) for i in range(2)]
        x3n = [sb(f"x3n{i}", [P, HID]) for i in range(2)]
        r_t = [sb(f"r_t{i}", [P, HID]) for i in range(2)]
        xf = [sb(f"xf{i}", [P, HID]) for i in range(2)]
        sg = [sb(f"sg{i}", [P, HID], BF16) for i in range(2)]
        pr = sb("pr", [P, HID], BF16)
        xm = sb("xm", [P, NTILE, DS])
        ts = sb("ts", [P, NTILE])
        cs = sb("cs", [P, 8])
        cm = sb("cm", [P, 8])
        top = sb("top", [P, 2])
        tk = sb("tk", [P, 2])
        pen = sb("pen", [P, NTILE])
        cand = sb("cand", [P, 2, NTILE])
        acc = sb("acc", [P, 2, NTILE])
        ohx = [sb(f"ohx{i}", [P, NTILE + DS]) for i in range(2)]
        ln = {n: (sb(f"st_{n}", [P, 6]), sb(f"mv_{n}", [P, 2]), sb(f"sd_{n}", [P, 1]), sb(f"rd_{n}", [P, 1]))
              for n in ("a", "b", "c", "d")}
        banks = [ctx.enter_context(nc.psum_tensor(f"bank{i}", [P, HID], F32)) for i in range(8)]
        ohx_d = nc.dram_tensor("ohx_d", (TILES, P, NTILE + DS), F32, kind="Internal").ap()

        USES = [("xT", 1), ("x2T", 2), ("aT", 4), ("qT", 3), ("kT", 3), ("ffn", 1), ("q", 2), ("k", 2), ("v", 2),
                ("sc0", 3), ("sc1", 3), ("sc2", 3), ("sc3", 3), ("wo", 4), ("kvu", 3), ("at", 3)]
        AT = {n: p for p, (n, _) in enumerate(USES)}
        filled = {n: sem(f"filled_{n}") for n, _ in USES}
        taken = {n: sem(f"taken_{n}") for n, _ in USES}

        def bank(name):
            return banks[AT[name] % 8]

        def num(t):
            return t[1] if t[0] is None else t[0] * 4 + t[1]

        def back(t, n):
            return (t[0], t[1] - n)

        def valid(t):
            return t[0] is not None or 0 <= t[1] < TILES

        def where(t):
            b = t[1] % 2
            i = (t[1] - b) // 2
            return b, (i if t[0] is None else t[0] * 2 + i)

        def stored_count(a):
            b = a[1] % 2
            n = (a[1] - b) // 2
            return n if a[0] is None else a[0] * 2 + n

        def user_before(name, step):
            p = AT[name]
            while True:
                p, step = (p - 8, step) if p >= 8 else (p + 8, back(step, 1))
                if step[0] is None and step[1] < 0:
                    return None
                n, s_ = USES[p]
                if valid(back(step, s_)):
                    return n, back(step, s_)

        high_ready = {n: sem(f"high_ready_{n}") for n in ("xT", "x2T", "aT")}
        names = ("w_loaded2", "part_loaded0", "part_loaded1", "part_used", "setup_dve", "setup_act", "setup_pool", "setup_pe",
                 "xa_ready", "x1b_ready", "x2_ready", "xb_ready", "rot_parts", "qk_ready", "kd_ready", "qd_ready",
                 "kvd_ready", "kvu_ready", "kv_ready", "rms_ready", "x3_ready", "x3n_ready", "r_ready",
                 "xf_normed", "xf_scaled", "xf_ready", "sg_ready", "ohx_ready", "scored")
        S = {n: sem(n) for n in names}
        sp_steps, qt_copied = sem("sp_steps2"), sem("qt_copied")
        x1_loaded = [sem(f"x1_loaded{i}") for i in range(2)]
        rot_loaded = [sem(f"rot_loaded{i}") for i in range(2)]
        r_stored = [sem(f"r_stored{i}") for i in range(2)]
        ohx_stored = [sem(f"ohx_stored{i}") for i in range(2)]
        var_ready = {n: sem(f"var_ready_{n}") for n in ln}
        sd_ready = {n: sem(f"sd_ready_{n}") for n in ln}

        region = ExitStack()
        block = region.enter_context(nc.Block())

        def steps(eng, body):
            for t in range(8):
                body((None, t))
            with eng.Fori(2, TILES // 4) as i:
                for u_ in range(4):
                    body((i, u_))
            for t in range(TILES, TILES + LAST_STAGE):
                body((None, t))

        @block.sync
        def _(sp):
            def held(sem_, value):
                wait(sp, sem_, value)
                sp.sem_inc(sp_steps, 1)

            for r, src in enumerate([w["factors"][r] for r in range(RANKS)] + [w[n] for n in ("Wq", "Wk", "Wv", "Wo")]):
                if r >= 2:
                    sp.wait_ge(S["part_used"], r - 1)
                sp.dma_start(w_part[r % 2], src.rearrange("(k p) n -> p k n", p=P)).then_inc(S[f"part_loaded{r % 2}"], 16)

            def body(t):
                a = t
                if valid(a):
                    s_ = a[1] % 2
                    b, i = where(a)
                    held(S["x2_ready"], num(a) - 1)
                    sp.dma_start(x1t[s_][:], x1_v[b, i]).then_inc(x1_loaded[s_], 16)
                a = back(t, 1)
                if valid(a):
                    s_ = a[1] % 2
                    b, i = where(a)
                    held(S["rot_parts"], num(a) - 1)
                    sp.dma_start(rot[s_][:], w["rot"][i]).then_inc(rot_loaded[s_], 16)
                a = back(t, 6)
                if valid(a):
                    s_ = a[1] % 2
                    b, i = where(a)
                    held(S["r_ready"], num(a) + 1)
                    sp.dma_start(out_v[b, i], r_t[s_][:]).then_inc(r_stored[s_], 16)
                    held(S["ohx_ready"], num(a) + 1)
                    sp.dma_start(ohx_d[num(a)], ohx[s_][:]).then_inc(ohx_stored[s_], 16)

            steps(sp, body)
            for s_ in range(2):
                sp.wait_ge(r_stored[s_], 16 * TILES // 2)
                sp.wait_ge(ohx_stored[s_], 16 * TILES // 2)

        @block.gpsimd
        def _(pool):
            nc.gpsimd.memset(ones[:], 1.0)
            nc.gpsimd.memset(kv[0][:], 0.0)
            nc.gpsimd.memset(kv[1][:], 0.0)
            nc.gpsimd.memset(acc[:], -BIG)
            pool.drain().then_inc(S["setup_pool"], 1)
            pool.wait_ge(S["setup_act"], 1)

            def body(t):
                a = back(t, 5)
                if valid(a):
                    s_ = a[1] % 2
                    wait(pool, S["x3n_ready"], num(a) + 1)
                    if a[0] is not None or a[1] >= 2:
                        pool.wait_ge(r_stored[s_], 16 * stored_count(a))
                    nc.gpsimd.tensor_tensor(r_t[s_][:], x3[s_][:], x3n[s_][:], ALU.add).then_inc(S["r_ready"], 1)
                a = t
                if valid(a):
                    s_ = a[1] % 2
                    wait(pool, S["xa_ready"], num(a) + 1)
                    nc.gpsimd.tensor_tensor(x1t[s_][:], x1t[s_][:], bias_b[:], ALU.add).then_inc(S["x1b_ready"], 1)
                a = back(t, 5)
                if valid(a):
                    s_ = a[1] % 2
                    wait(pool, S["xf_normed"], num(a) + 1)
                    nc.gpsimd.tensor_tensor(xf[s_][:], xf[s_][:], gamma_b[:], ALU.mult).then_inc(S["xf_scaled"], 1)
                    wait(pool, S["xf_scaled"], num(a) + 1)
                    nc.gpsimd.tensor_tensor(xf[s_][:], xf[s_][:], beta_b[:], ALU.add).then_inc(S["xf_ready"], 1)
                a = back(t, 2)
                if valid(a):
                    s_ = a[1] % 2
                    wait(pool, S["rot_parts"], num(a) + 1)
                    turned = qk[s_][:].rearrange("p q (h z j) -> p (q h) z j", h=HEADS, z=2)[:, :, :, 0:ROT]
                    nc.gpsimd.tensor_tensor(turned, rc[:], rs_[:], ALU.add).then_inc(S["qk_ready"], 1)
                    wait(pool, S["qk_ready"], num(a) + 1)
                    wait(pool, filled["kvu"], num(a) - 1)
                    nc.gpsimd.tensor_tensor(kd[s_][:].rearrange("p (h d) -> p h d", h=HEADS),
                                            qk[s_][:, 1, :].rearrange("p (h d) -> p h d", h=HEADS),
                                            k_dec[:].unsqueeze(2).to_broadcast([P, HEADS, HD]), ALU.mult
                                            ).then_inc(S["kd_ready"], 1)
                a = back(t, 3)
                if valid(a):
                    b = a[1] % 2
                    wait(pool, S["kv_ready"], num(a))
                    nc.gpsimd.tensor_tensor(kvd[:], kv[b][:], kv_dec[:], ALU.mult).then_inc(S["kvd_ready"], 1)
                    wait(pool, S["kvd_ready"], num(a) + 1)
                    wait(pool, S["kvu_ready"], num(a) + 1)
                    wait(pool, filled["at"], num(a) + 1)
                    nc.gpsimd.tensor_tensor(kv[b][:], kvd[:], kvu[:], ALU.add).then_inc(S["kv_ready"], 1)

            steps(pool, body)

        @block.scalar
        def _(act):
            for dst, src in ((rms_w, w["rms_w"]), (ident, w["eye"]), (decay, w["decay"]), (q_dec, w["q_dec"]),
                             (k_dec, w["k_dec"]), (kv_dec, w["kv_dec"]), (kv_mask, w["kv_mask"]),
                             (tie8, w["tie8"]), (tie64, w["tie64"]), (grid16, w["grid16"]), (oscale, w["oscale"])):
                act.dma_start(dst[:], src).then_inc(S["w_loaded2"], 16)
            for dst, src in ((bias_b, w["bias"]), (gamma_b, w["gamma"]), (beta_b, w["beta"])):
                act.dma_start(dst[:], src.to_broadcast([P, HID])).then_inc(S["w_loaded2"], 16)
            act.dma_start(tab[:, 0, :], w["bases"].rearrange("a j g -> a (j g)")).then_inc(S["w_loaded2"], 16)
            act.dma_start(tab[:, 1, :], w["slopes"].rearrange("a j g -> a (j g)")).then_inc(S["w_loaded2"], 16)
            act.wait_ge(S["setup_dve"], 1)
            nc.scalar.activation(smean[:], smean[:], ACT.Sign).then_inc(S["setup_act"], 1)
            act.wait_ge(S["setup_pe"], 1)
            nc.scalar.copy(sign_b[:], banks[0][:]).then_inc(S["setup_act"], 1)

            def take(name, a, dst, view=lambda p: p[:]):
                act.wait_ge(filled[name], num(a) + 1)
                nc.scalar.copy(dst, view(bank(name))).then_inc(taken[name], 1)

            def take_high(name, a, parts):
                act.wait_ge(filled[name], num(a) + 1)
                nc.scalar.copy(parts[0][:].rearrange("p k n -> p (k n)"), bank(name)[:]).then_inc(high_ready[name], 1)

            def root(n, a, lag):
                wait(act, var_ready[n], num(a) + 1)
                nc.scalar.activation(ln[n][2][:], ln[n][1][:, 1:2], ACT.Sqrt, bias=LN_EPS).then_inc(sd_ready[n], 1)

            flat = "p (k n) -> p k n"

            def body(t):
                if valid(back(t, 1)):
                    a = back(t, 1)
                    wait(act, filled["ffn"], num(a))
                    take_high("xT", a, xaT)
                if valid(back(t, 2)):
                    a = back(t, 2)
                    wait(act, filled["v"], num(a))
                    take_high("x2T", a, xbT)
                if valid(back(t, 5)):
                    root("c", back(t, 5), 5)
                if valid(back(t, 4)):
                    a = back(t, 4)
                    wait(act, filled["wo"], num(a))
                    take_high("aT", a, aTs)
                if valid(back(t, 3)):
                    a = back(t, 3)
                    wait(act, filled["sc3"], num(a))
                    act.wait_ge(filled["qT"], num(a) + 1)
                    nc.scalar.copy(qTs[:].rearrange("p k n -> p (k n)"), bank("qT")[:]).then_inc(qt_copied, 1)
                    take("kT", a, kTs[:].rearrange("p k n -> p (k n)"))
                if valid(t):
                    root("a", t, 0)
                if valid(back(t, 5)):
                    root("d", back(t, 5), 5)
                if valid(back(t, 2)):
                    a = back(t, 2)
                    s_ = a[1] % 2
                    wait(act, filled["kT"], num(a) - 1)
                    wait(act, S["kd_ready"], num(a) - 1)
                    take("q", a, qk[s_][:, 0, :])
                    take("k", a, qk[s_][:, 1, :])
                    wait(act, filled["at"], num(a) - 1)
                    take("v", a, vv[s_][:])
                if valid(back(t, 1)):
                    root("b", back(t, 1), 1)
                if valid(back(t, 5)):
                    a = back(t, 5)
                    wait(act, S["xf_ready"], num(a) + 1)
                    wait(act, S["scored"], num(a) - 1)
                    nc.scalar.activation(sg[a[1] % 2][:], xf[a[1] % 2][:], ACT.Sign).then_inc(S["sg_ready"], 1)
                if valid(back(t, 3)):
                    a = back(t, 3)
                    s_ = a[1] % 2
                    act.drain()
                    act.wait_ge(filled["at"], num(a) + 1)
                    wait(act, S["x3_ready"], num(a) - 1)
                    nc.scalar.activation(junk[:], bank("at")[:], ACT.Square, accum_out=rsum[s_][:])
                    nc.scalar.copy(at_s[s_][:], bank("at")[:])
                    act.drain().then_inc(taken["at"], 1)
                    nc.scalar.activation(rsum[s_][:], rsum[s_][:], ACT.Sqrt, bias=RMS_EPS, scale=1.0 / HID
                                         ).then_inc(S["rms_ready"], 1)

            steps(act, body)

        @block.vector
        def _(dve):
            dve.wait_ge(S["w_loaded2"], 16 * 16)
            dve.wait_ge(S["setup_pool"], 1)
            nc.vector.tensor_reduce(smean[:], tab[:, 1, :].rearrange("a (j g) -> a j g", g=GRID), AX.X, ALU.add
                                    ).then_inc(S["setup_dve"], 1)
            dve.wait_ge(S["setup_act"], 1)
            nc.vector.tensor_tensor(sdiag, ident[0:NTILE, 0:NTILE].unsqueeze(2).to_broadcast([NTILE, NTILE, DS]),
                                    smean[:].unsqueeze(1).to_broadcast([NTILE, NTILE, DS]), ALU.mult
                                    ).then_inc(S["setup_dve"], 1)
            nc.vector.tensor_scalar(tab[:], tab[:], oscale[:], None, ALU.mult)

            def loaded(r):
                dve.wait_ge(S[f"part_loaded{r % 2}"], 16 * (r // 2 + 1))

            def split(n, w_):
                nc.vector.tensor_copy(w_high[n][:], w_)
                dve.drain()
                return nc.vector.tensor_tensor(w_low[n][:], w_, w_high[n][:], ALU.subtract)

            for r in range(RANKS):
                loaded(r)
                if r == 0:
                    nc.vector.tensor_copy(w_sum, w_part[0]).then_inc(S["part_used"], 1)
                else:
                    dve.wait_ge(S["part_used"], r)
                    nc.vector.tensor_tensor(w_sum, w_sum, w_part[r % 2], ALU.add).then_inc(S["part_used"], 1)
            dve.drain()
            split("f", w_sum)
            for i, n in enumerate(("q", "k", "v", "o")):
                loaded(RANKS + i)
                part = w_part[(RANKS + i) % 2]
                if n == "o":
                    for k in range(KB):
                        nc.vector.tensor_scalar(part[:, k, :], part[:, k, :], rms_w[:, k:k + 1], None, ALU.mult)
                    dve.drain()
                split(n, part).then_inc(S["part_used"], 1)
            dve.drain().then_inc(S["setup_dve"], 1)
            dve.wait_ge(S["setup_act"], 2)

            def stats(n, x_):
                nc.vector.bn_stats(ln[n][0][:], x_)
                dve.drain()
                nc.vector.bn_aggr(ln[n][1][:], ln[n][0][:]).then_inc(var_ready[n], 1)

            def norm(n, a, x_, dst, done):
                dve.wait_ge(sd_ready[n], num(a) + 1)
                nc.vector.reciprocal(ln[n][3][:], ln[n][2][:])
                dve.drain()
                nc.vector.tensor_scalar(dst, x_, ln[n][1][:, 0:1], ln[n][3][:], ALU.subtract, ALU.mult).then_inc(done, 1)

            def low(name, a, parts):
                dve.wait_ge(high_ready[name], num(a) + 1)
                nc.vector.tensor_tensor(parts[1][:].rearrange("p k n -> p (k n)"), bank(name)[:],
                                        parts[0][:].rearrange("p k n -> p (k n)"), ALU.subtract
                                        ).then_inc(taken[name], 1)

            def score(a):
                s_ = a[1] % 2
                oh = ohx[s_][:, 0:NTILE]
                xs = ohx[s_][:, NTILE:NTILE + DS]
                dve.wait_ge(S["sg_ready"], num(a) + 1)
                nc.vector.tensor_tensor(pr[:], sg[s_][:], sign_b[:], ALU.mult)
                dve.drain()
                nc.vector.tensor_reduce(ts[:], pr[:].rearrange("p (i j) -> p i j", j=DS), AX.X, ALU.add)
                dve.drain()
                nc.vector.tensor_reduce(cs[:], ts[:].rearrange("p (c i) -> p c i", c=NCL), AX.X, ALU.add)
                dve.drain()
                nc.vector.scalar_tensor_tensor(cs[:], cs[:], 8.0, tie8[:], ALU.mult, ALU.add)
                nc.vector.scalar_tensor_tensor(ts[:], ts[:], 8.0, tie64[:], ALU.mult, ALU.add)
                dve.drain()
                nc.vector.tensor_reduce(top[:, 0:1], cs[:], AX.X, ALU.max)
                dve.drain()
                nc.vector.tensor_scalar(cm[:], cs[:], top[:, 0:1], 1024.0, ALU.is_equal, ALU.mult)
                dve.drain()
                nc.vector.tensor_tensor(ts[:].rearrange("p (c i) -> p c i", c=NCL),
                                        ts[:].rearrange("p (c i) -> p c i", c=NCL),
                                        cm[:].unsqueeze(2).to_broadcast([P, NCL, 8]), ALU.add)
                dve.drain()
                nc.vector.tensor_reduce(top[:, 1:2], ts[:], AX.X, ALU.max)
                if a[0] is not None or a[1] >= 2:
                    dve.drain()
                    dve.wait_ge(ohx_stored[s_], 16 * stored_count(a))
                else:
                    dve.drain()
                nc.vector.tensor_scalar(oh, ts[:], top[:, 1:2], None, ALU.is_equal)
                dve.drain()
                nc.vector.tensor_tensor(xm[:], xf[s_][:].rearrange("p (i j) -> p i j", j=DS),
                                        oh.unsqueeze(2).to_broadcast([P, NTILE, DS]), ALU.mult)
                nc.vector.tensor_scalar(pen[:], oh, -1.0, BIG, ALU.add, ALU.mult)
                dve.drain()
                nc.vector.tensor_reduce(xs, xm[:].rearrange("p i j -> p j i"), AX.X, ALU.add)
                dve.drain()
                nc.vector.tensor_reduce(tk[:, 0:1], xs, AX.X, ALU.max)
                nc.vector.tensor_reduce(tk[:, 1:2], xs, AX.X, ALU.min, negate=True)
                dve.drain()
                for q in range(2):
                    nc.vector.scalar_tensor_tensor(cand[:, q, :], oh, tk[:, q:q + 1], pen[:], ALU.mult, ALU.add)
                dve.drain().then_inc(S["ohx_ready"], 1)
                nc.vector.tensor_tensor(acc[:], acc[:], cand[:], ALU.max).then_inc(S["scored"], 1)

            def body(t):
                s5, s3, s2, s1, s4 = back(t, 5), back(t, 3), back(t, 2), back(t, 1), back(t, 4)
                if valid(s1):
                    low("xT", s1, xaT)
                if valid(s5):
                    stats("c", x3[s5[1] % 2][:])
                if valid(s2):
                    low("x2T", s2, xbT)
                if valid(s4):
                    low("aT", s4, aTs)
                if valid(s3):
                    dve.wait_ge(filled["qT"], num(s3) + 1)
                    dve.wait_ge(qt_copied, num(s3) + 1)
                    wait(dve, filled["at"], num(s3))
                    nc.vector.tensor_tensor(qdT[:].rearrange("p k n -> p (k n)"), bank("qT")[:],
                                            q_dec[:].rearrange("p k n -> p (k n)"), ALU.mult).then_inc(taken["qT"], 1)
                if valid(t):
                    dve.wait_ge(x1_loaded[t[1] % 2], 16 * (stored_count(t) + 1))
                    stats("a", x1t[t[1] % 2][:])
                if valid(s5):
                    s_ = s5[1] % 2
                    wait(dve, S["r_ready"], num(s5) - 1)
                    norm("c", s5, x3[s_][:], x3n[s_][:], S["x3n_ready"])
                    dve.drain()
                    stats("d", x3n[s_][:])
                if valid(back(t, 6)):
                    score(back(t, 6))
                if valid(t):
                    wait(dve, filled["xT"], num(t) - 1)
                    norm("a", t, x1t[t[1] % 2][:], xa[t[1] % 2][:], S["xa_ready"])
                if valid(s5):
                    norm("d", s5, x3n[s5[1] % 2][:], xf[s5[1] % 2][:], S["xf_normed"])
                if valid(s1):
                    dve.wait_ge(filled["ffn"], num(s1) + 1)
                    dve.wait_ge(S["x1b_ready"], num(s1) + 1)
                    nc.vector.scalar_tensor_tensor(x2[s1[1] % 4][:], bank("ffn")[:], float(RANKS) ** -0.5,
                                                   x1t[s1[1] % 2][:], ALU.mult, ALU.add)
                    dve.drain().then_inc(taken["ffn"], 1)
                    nc.vector.bn_stats(ln["b"][0][:], x2[s1[1] % 4][:]).then_inc(S["x2_ready"], 1)
                    dve.drain()
                    nc.vector.bn_aggr(ln["b"][1][:], ln["b"][0][:]).then_inc(var_ready["b"], 1)
                if valid(s2):
                    s_ = s2[1] % 2
                    dve.wait_ge(taken["k"], num(s2) + 1)
                    dve.wait_ge(rot_loaded[s_], 16 * (stored_count(s2) + 1))
                    wait(dve, S["qk_ready"], num(s2))
                    pairs = qk[s_][:].rearrange("p q (h z j) -> p (q h) z j", h=HEADS, z=2)[:, :, :, 0:ROT]
                    cos = rot[s_][:, 0, :].rearrange("p (z j) -> p z j", z=2)
                    sin = rot[s_][:, 1, :].rearrange("p (z j) -> p z j", z=2)
                    nc.vector.tensor_tensor(rc[:], pairs, cos.unsqueeze(1).to_broadcast([P, 2 * HEADS, 2, ROT]), ALU.mult)
                    for z in range(2):
                        last_ = nc.vector.tensor_tensor(
                            rs_[:, :, z, :], pairs[:, :, 1 - z, :],
                            sin[:, z, :].unsqueeze(1).to_broadcast([P, 2 * HEADS, ROT]), ALU.mult)
                    dve.drain().then_inc(S["rot_parts"], 1)
                if valid(s1):
                    wait(dve, filled["x2T"], num(s1) - 1)
                    norm("b", s1, x2[s1[1] % 4][:], xb[s1[1] % 2][:], S["xb_ready"])
                if valid(s3):
                    wait(dve, filled["at"], num(s3))
                    for r in range(4):
                        dve.wait_ge(filled[f"sc{r}"], num(s3) + 1)
                        nc.vector.tensor_tensor(scm[:, r, :, :].rearrange("p k n -> p (k n)"), bank(f"sc{r}")[:],
                                                decay[:, r, :, :].rearrange("p k n -> p (k n)"), ALU.mult
                                                ).then_inc(taken[f"sc{r}"], 1)
                if valid(s4):
                    s_ = s4[1] % 2
                    dve.wait_ge(S["rms_ready"], num(s4) + 1)
                    nc.vector.reciprocal(rrms[s_][:], rsum[s_][:])
                    dve.drain()
                    dve.wait_ge(filled["wo"], num(s4) + 1)
                    wait(dve, S["r_ready"], num(s4) - 1)
                    nc.vector.scalar_tensor_tensor(x3[s_][:], bank("wo")[:], rrms[s_][:], x2[s4[1] % 4][:],
                                                   ALU.mult, ALU.add).then_inc(taken["wo"], 1)
                    dve.drain().then_inc(S["x3_ready"], 1)
                if valid(s3):
                    dve.wait_ge(filled["kvu"], num(s3) + 1)
                    wait(dve, S["kv_ready"], num(s3))
                    nc.vector.tensor_tensor(kvu[:].rearrange("p k n -> p (k n)"), bank("kvu")[:],
                                            kv_mask[:].rearrange("p k n -> p (k n)"), ALU.mult
                                            ).then_inc(taken["kvu"], 1)
                    dve.wait_ge(taken["kvu"], num(s3) + 1)
                    dve.sem_inc(S["kvu_ready"], 1)

            steps(dve, body)

        @block.tensor
        def _(pe):
            pe.wait_ge(S["setup_dve"], 2)
            nc.tensor.matmul(banks[0][:], ones[0:NTILE, :], sdiag.rearrange("a i j -> a (i j)"),
                             start=True, stop=True).then_inc(S["setup_pe"], 1)
            pe.wait_ge(S["setup_dve"], 3)
            pe.wait_ge(S["setup_act"], 2)

            def free(name, t):
                before = user_before(name, t)
                if before is not None:
                    pe.wait_ge(taken[before[0]], num(before[1]) + 1)
                return bank(name)

            def turn(name, t, src):
                b_ = free(name, t)
                for k in range(KB):
                    last_ = nc.tensor.transpose(b_[:, k * P:(k + 1) * P], src[:, k * P:(k + 1) * P], ident[:])
                last_.then_inc(filled[name], 1)

            def product(name, t, src, n):
                b_ = free(name, t)
                for k in range(KB):
                    for i, (part, wt) in enumerate(((0, w_high[n][:, k, :]), (0, w_low[n][:, k, :]),
                                                    (1, w_high[n][:, k, :]))):
                        last_ = nc.tensor.matmul(b_[:], src[part][:, k, :], wt,
                                                 start=(k == 0 and i == 0), stop=(k == KB - 1 and i == 2))
                last_.then_inc(filled[name], 1)

            def body(t):
                s1, s2, s3, s4 = back(t, 1), back(t, 2), back(t, 3), back(t, 4)
                if valid(s1):
                    pe.wait_ge(S["xa_ready"], num(s1) + 1)
                    turn("xT", t, xa[s1[1] % 2])
                if valid(s2):
                    pe.wait_ge(S["xb_ready"], num(s2) + 1)
                    turn("x2T", t, xb[s2[1] % 2])
                if valid(s4):
                    pe.wait_ge(taken["at"], num(s4) + 1)
                    turn("aT", t, at_s[s4[1] % 2])
                if valid(s3):
                    pe.wait_ge(S["qk_ready"], num(s3) + 1)
                    turn("qT", t, qk[s3[1] % 2][:, 0, :])
                    turn("kT", t, qk[s3[1] % 2][:, 1, :])
                if valid(s1):
                    pe.wait_ge(taken["xT"], num(s1) + 1)
                    product("ffn", t, xaT, "f")
                if valid(s2):
                    pe.wait_ge(taken["x2T"], num(s2) + 1)
                    for name in ("q", "k", "v"):
                        product(name, t, xbT, name)
                if valid(s3):
                    pe.wait_ge(qt_copied, num(s3) + 1)
                    pe.wait_ge(taken["kT"], num(s3) + 1)
                    for r in range(4):
                        free(f"sc{r}", t)
                    for g in range(HG):
                        for r in range(4):
                            rows = slice(HD * r, HD * r + HD)
                            last_ = nc.tensor.matmul(bank(f"sc{r}")[:, g * P:(g + 1) * P], kTs[rows, g, :],
                                                     qTs[rows, g, :], start=True, stop=True,
                                                     tile_position=(HD * r, 0))
                            if g == HG - 1:
                                last_.then_inc(filled[f"sc{r}"], 1)
                if valid(s4):
                    pe.wait_ge(taken["aT"], num(s4) + 1)
                    product("wo", t, aTs, "o")
                if valid(s3):
                    s_ = s3[1] % 2
                    pe.wait_ge(S["kd_ready"], num(s3) + 1)
                    pe.wait_ge(taken["v"], num(s3) + 1)
                    b_ = free("kvu", t)
                    for g in range(HG):
                        cols = slice(g * P, (g + 1) * P)
                        last_ = nc.tensor.matmul(b_[:, cols], kd[s_][:, cols], vv[s_][:, cols],
                                                 start=(g == 0), stop=(g == HG - 1), skip_group_check=True)
                    last_.then_inc(filled["kvu"], 1)
                    pe.wait_ge(taken["qT"], num(s3) + 1)
                    if s3[0] is not None or s3[1] >= 2:
                        pe.wait_ge(S["kv_ready"], num(s3) - 1)
                    b_ = free("at", t)
                    for g in range(HG):
                        cols = slice(g * P, (g + 1) * P)
                        nc.tensor.matmul(b_[:, cols], qdT[:, g, :], kv[s_][:, g, :], start=(g == 0), stop=False,
                                         skip_group_check=True)
                    for r in range(4):
                        pe.wait_ge(taken[f"sc{r}"], num(s3) + 1)
                        for g in range(HG):
                            cols = slice((4 * g + r) * HD, (4 * g + r + 1) * HD)
                            last_ = nc.tensor.matmul(b_[:, cols], scm[:, r, g, :], vv[s_][:, cols], start=False,
                                                     stop=(r == 3 and g == HG - 1), skip_group_check=True)
                    last_.then_inc(filled["at"], 1)

            steps(pe, body)

        region.close()
        finish(nc, out_v, ohx_d, dict(
            R=w_part, od=decay[:].rearrange("p r g n -> p r (g n)"),
            eq=x1t[0][:].rearrange("p (t g) -> p t g", g=GRID), prod=qk_all, banks=banks,
            ident=ident, ones=ones, tab=tab, grid16=grid16, acc=acc,
            oq=[v[:, 0:4 * (NTILE + DS)].rearrange("p (t n) -> p t n", t=4) for v in vv], ohTs=junk[0:NTILE, :],
            ext_T=sb("ext_T", [P, 1]), ext_diag=kTs[:, 0, :], ext=kTs[:, 1, :].rearrange("p (q t) -> p q t", q=2),
            e=sb("e", [P, 2, 4]), rdn=sb("rdn", [P, 4]), gi=sb("gi", [P, 4, DS], I32),
            **{n: kTs[:, 2 + i // 4, 4 * DS * (i % 4):4 * DS * (i % 4 + 1)].rearrange("p (t j) -> p t j", t=4)
               for i, n in enumerate(("v16", "gf", "gt", "bsel", "ssel"))}), NTILE, DS, GRID, TILES)


def finish(nc, out_v, ohx_d, buf, NTILE, DS, GRID, TILES):
    N = 4
    R, od, eq, prod, banks = buf["R"], buf["od"], buf["eq"], buf["prod"], buf["banks"]
    oq, ident, ones, tab, grid16 = buf["oq"], buf["ident"], buf["ones"], buf["tab"], buf["grid16"]
    acc, ext_T, ext_diag, ext = buf["acc"], buf["ext_T"], buf["ext_diag"], buf["ext"]
    ohTs, e, rdn, v16, gi, gf, gt, bsel, ssel = (buf[n] for n in (
        "ohTs", "e", "rdn", "v16", "gi", "gf", "gt", "bsel", "ssel"))
    ctx = ExitStack()
    with ctx:
        def sem(name):
            return ctx.enter_context(nc.semaphore(name))

        ext_step, ext_pe = sem("ext_step"), sem("ext_pe")
        r_loaded = [sem(f"r_loaded{i}") for i in range(2)]
        oq_loaded = [sem(f"oq_loaded{i}") for i in range(2)]
        out_stored = [sem(f"out_stored{i}") for i in range(2)]
        turned, ohT_ready, looked_up, looked_taken = sem("turned3"), sem("ohT_ready"), sem("looked_up"), sem("looked_taken")
        od_ready, out_ready, sp_steps3, pe_steps3 = (
            sem("od_ready"), sem("out_ready"), sem("sp_steps3"), sem("pe_steps3"))
        block = ctx.enter_context(nc.Block())
        GROUPS = TILES // N

        def groups(eng, body):
            for v in range(2):
                body(v, v, 0)
            with eng.Fori(1, GROUPS // 2) as i:
                for v in range(2):
                    body(i * 2 + v, v, i)

        @block.sync
        def _(sp):
            def load(G, v, i):
                wait(sp, out_stored[v], i * 32)
                sp.sem_inc(sp_steps3, 1)
                for b in range(2):
                    sp.dma_start(R[v][:, b::2, :], out_v[b, bass.ds(G * 2, 2)].rearrange("i p d -> p i d")
                                 ).then_inc(r_loaded[v], 16)
                sp.dma_start(oq[v][:], ohx_d[bass.ds(G * N, N)].rearrange("t p n -> p t n")).then_inc(oq_loaded[v], 16)

            def store(G, v, i):
                wait(sp, out_ready, G + 1)
                sp.sem_inc(sp_steps3, 1)
                for b in range(2):
                    sp.dma_start(out_v[b, bass.ds(G * 2, 2)].rearrange("i p d -> p i d"), R[v][:, b::2, :]
                                 ).then_inc(out_stored[v], 16)

            load(0, 0, 0)
            load(1, 1, 0)
            with sp.Fori(0, GROUPS // 2 - 1) as i:
                for v in range(2):
                    store(i * 2 + v, v, i)
                    load(i * 2 + (v + 2), v, i + 1)
            for v in range(2):
                store(GROUPS - 2 + v, v, 0)
            for v in range(2):
                sp.wait_ge(out_stored[v], 32 * (GROUPS // 2))

        @block.gpsimd
        def _(pool):
            def body(G, v, i):
                pool.wait_ge(od_ready, G + 1)
                pool.wait_ge(r_loaded[v], i * 32 + 32)
                nc.gpsimd.tensor_tensor(R[v][:], R[v][:], od[:], ALU.add).then_inc(out_ready, 1)

            groups(pool, body)

        @block.scalar
        def _(act):
            def body(G, v, i):
                act.wait_ge(turned, G + 1)
                wait(act, looked_up, G)
                nc.scalar.copy(ohTs[:], banks[0][0:NTILE, :]).then_inc(ohT_ready, 1)

            groups(act, body)

        @block.vector
        def _(dve):
            dve.wait_ge(ext_pe, 1)
            nc.vector.tensor_reduce(ext_T[:], banks[0][:, 0:P], AX.X, ALU.max)
            dve.drain()
            nc.vector.tensor_scalar(ext_diag[:], ident[:], ext_T[:], None, ALU.mult).then_inc(ext_step, 1)
            dve.wait_ge(ext_pe, 2)
            nc.vector.tensor_copy(ext[:].rearrange("p q i -> p (q i)"), banks[1][:, 0:P]).then_inc(ext_step, 1)
            dve.wait_ge(ext_step, 2)

            def body(G, v, i):
                dve.wait_ge(oq_loaded[v], i * 16 + 16)
                oh = oq[v][:, :, 0:NTILE]
                xs = oq[v][:, :, NTILE:NTILE + DS]
                for q in range(2):
                    nc.vector.tensor_tensor(prod[:, q, 0:N * NTILE].rearrange("p (t i) -> p t i", t=N), oh,
                                            ext[:, q, :].unsqueeze(1).to_broadcast([P, N, NTILE]), ALU.mult)
                dve.drain()
                for q in range(2):
                    nc.vector.tensor_reduce(e[:, q, :], prod[:, q, 0:N * NTILE].rearrange("p (t i) -> p t i", t=N),
                                            AX.X, ALU.add)
                dve.drain()
                nc.vector.tensor_tensor(rdn[:], e[:, 0, :], e[:, 1, :], ALU.add)
                nc.vector.tensor_tensor(v16[:], xs, e[:, 1, :].unsqueeze(2).to_broadcast([P, N, DS]), ALU.add)
                dve.drain()
                nc.vector.tensor_scalar_add(rdn[:], rdn[:], 1e-8)
                dve.drain()
                nc.vector.reciprocal(rdn[:], rdn[:])
                dve.drain()
                nc.vector.tensor_tensor(v16[:], v16[:], rdn[:].unsqueeze(2).to_broadcast([P, N, DS]), ALU.mult)
                dve.drain()
                nc.vector.tensor_scalar(v16[:], v16[:], 0.0, 1.0 - 1e-6, ALU.max, ALU.min)
                dve.drain()
                nc.vector.tensor_scalar(v16[:], v16[:], float(GRID), None, ALU.mult)
                dve.drain()
                nc.vector.tensor_copy(gi[:], v16[:])
                dve.drain()
                nc.vector.tensor_copy(gf[:], gi[:])
                dve.drain()
                nc.vector.tensor_tensor(gt[:], gf[:], v16[:], ALU.is_gt)
                dve.drain()
                nc.vector.tensor_tensor(gf[:], gf[:], gt[:], ALU.subtract)
                dve.drain()
                nc.vector.tensor_tensor(v16[:], v16[:], gf[:], ALU.subtract)
                cell = gf[:].rearrange("p t j -> p (t j)").unsqueeze(2).to_broadcast([P, N * DS, GRID])
                nc.vector.tensor_tensor(eq, cell, grid16[:].unsqueeze(1).to_broadcast([P, N * DS, GRID]), ALU.is_equal)
                dve.drain()
                dve.wait_ge(looked_up, G + 1)
                for q in range(2):
                    nc.vector.tensor_tensor(prod[:, q, :].rearrange("p (t g) -> p t g", g=GRID), eq,
                                            banks[1 + q][:].rearrange("p (t g) -> p t g", g=GRID), ALU.mult)
                dve.drain().then_inc(looked_taken, 1)
                for q, dst in ((0, bsel), (1, ssel)):
                    nc.vector.tensor_reduce(dst[:].rearrange("p t j -> p (t j)"),
                                            prod[:, q, :].rearrange("p (t g) -> p t g", g=GRID), AX.X, ALU.add)
                dve.drain()
                nc.vector.tensor_tensor(ssel[:], ssel[:], v16[:], ALU.mult)
                dve.drain()
                nc.vector.tensor_tensor(bsel[:], bsel[:], ssel[:], ALU.add)
                dve.drain()
                wait(dve, out_ready, G)
                nc.vector.tensor_tensor(od[:].rearrange("p t (i j) -> p t i j", j=DS),
                                        oh.unsqueeze(3).to_broadcast([P, N, NTILE, DS]),
                                        bsel[:].unsqueeze(2).to_broadcast([P, N, NTILE, DS]), ALU.mult
                                        ).then_inc(od_ready, 1)

            groups(dve, body)

        @block.tensor
        def _(pe):
            nc.tensor.transpose(banks[0][:, 0:P], acc[:].rearrange("p q i -> p (q i)"), ident[:]).then_inc(ext_pe, 1)
            pe.wait_ge(ext_step, 1)
            nc.tensor.matmul(banks[1][:, 0:P], ones[:], ext_diag[:], start=True, stop=True).then_inc(ext_pe, 1)
            pe.wait_ge(ext_step, 2)

            def body(G, v, i):
                pe.wait_ge(oq_loaded[v], i * 16 + 16)
                wait(pe, ohT_ready, G)
                pe.sem_inc(pe_steps3, 1)
                for t in range(N):
                    last_ = nc.tensor.transpose(banks[0][0:NTILE, t * P:(t + 1) * P], oq[v][:, t, 0:NTILE], ident[:])
                last_.then_inc(turned, 1)
                pe.wait_ge(ohT_ready, G + 1)
                wait(pe, looked_taken, G)
                for q in range(2):
                    for t in range(N):
                        last_ = nc.tensor.matmul(banks[1 + q][:, t * P:(t + 1) * P], ohTs[:, t * P:(t + 1) * P],
                                                 tab[:, q, :], start=True, stop=True)
                last_.then_inc(looked_up, 1)

            groups(pe, body)


def constants():
    f32 = np.float32
    H, D, C, T_ = 16, 32, 128, 4096
    start = 2.0 ** (-2.0 ** (-(np.log2(H) - 3)))
    slopes = np.array([start * start ** i for i in range(H)], f32)
    r = np.exp(-slopes).astype(f32).astype(np.float64)
    i = np.arange(C, dtype=np.float64)
    diff = i[None, :] - i[:, None]
    full = np.where(diff[None] >= 0, r[:, None, None] ** np.maximum(diff, 0)[None], 0.0)
    decay = full.reshape(4, 4, C, C).transpose(2, 1, 0, 3)
    q_dec = (r[:, None] ** (i[None, :] + 1)).reshape(4, 4, C)
    q_dec = np.repeat(q_dec.transpose(1, 0, 2), D, axis=0)
    k_dec = (r[:, None] ** (C - 1 - i[None, :])).T
    kv_mask = np.kron(np.eye(4), np.ones((D, D)))
    kv_dec = np.stack([kv_mask * np.repeat(r.reshape(4, 4)[g] ** float(C), D)[:, None] for g in range(4)], 1)
    freq = (f32(1.0 / 1024.0) ** np.linspace(0.0, 1.0, D // 4, dtype=f32)).astype(f32)
    theta = (np.arange(T_, dtype=f32)[:, None] * freq[None, :]).astype(f32)
    cos, sin = np.cos(theta.astype(np.float64)), np.sin(theta.astype(np.float64))
    rot = np.stack([np.concatenate([cos, cos], 1), np.concatenate([sin, -sin], 1)], 1)
    out = {
        "eye": np.eye(128), "decay": decay, "q_dec": q_dec, "k_dec": k_dec, "kv_dec": kv_dec,
        "kv_mask": np.broadcast_to(kv_mask[:, None], (128, 4, 128)), "rot": rot.reshape(T_ // 128, 128, 2, 16),
        "tie8": np.broadcast_to(7.0 - np.arange(8), (128, 8)),
        "tie64": np.broadcast_to(7.0 - np.arange(64) % 8, (128, 64)),
        "grid16": np.broadcast_to(np.arange(16.0), (128, 16)),
    }
    return {k: np.ascontiguousarray(v.astype(f32)) for k, v in out.items()}


def kernel(**inputs):
    import numpy as _np
    import concourse.bacc as _bacc
    from concourse import mybir as _mybir
    from concourse.bass_utils import run_bass_kernel_spmd as _run

    nc = _bacc.Bacc("TRN2", target_bir_lowering=False, num_devices=1)
    a = {k: _np.ascontiguousarray(v) for k, v in inputs.items()}
    const = constants()

    def per_group(v):
        return v.reshape(-1, 128, v[0].size).transpose(1, 0, 2)

    arrays = {
        "x": a["L0_attn_x"], "in_w": a["L0_attn_in_proj_w"], "xproj_w": a["L0_attn_x_proj_w"],
        "dt_w": a["L0_attn_dt_proj_w"], "out_w": a["L0_attn_out_proj_w"],
        "chan": _np.ascontiguousarray(_np.concatenate([
            per_group(a["L0_attn_conv_w"]), per_group(a["L0_attn_conv_b"]), per_group(a["L0_attn_D_param"]),
            per_group(a["L0_attn_dt_proj_b"]), per_group(a["L0_attn_A_log"])], axis=2)),
        "factors": a["L0_ffn_factors"], "bias": a["L0_ffn_bias"].reshape(1, -1),
        "Wq": a["L1_attn_Wq"], "Wk": a["L1_attn_Wk"], "Wv": a["L1_attn_Wv"], "Wo": a["L1_attn_Wo"],
        "rms_w": _np.ascontiguousarray(a["L1_attn_rms_w"].reshape(-1, 128).T),
        "gamma": a["L1_ffn_ln_gamma"].reshape(1, -1), "beta": a["L1_ffn_ln_beta"].reshape(1, -1),
        "bases": a["L1_ffn_spline_bases"], "slopes": a["L1_ffn_spline_slopes"],
        "oscale": a["L1_ffn_output_scale"].reshape(-1, 1),
        **const,
    }
    w = {k: nc.dram_tensor(f"in_{k}", v.shape, _mybir.dt.from_np(v.dtype), kind="ExternalInput").ap()
         for k, v in arrays.items()}
    shape = a["L0_attn_x"].shape
    x1 = nc.dram_tensor("x1", shape, F32, kind="Internal").ap()
    out = nc.dram_tensor("out_0", shape, F32, kind="ExternalOutput").ap()
    mamba_block(nc, w["x"], w["in_w"], w["chan"], w["xproj_w"], w["dt_w"], w["out_w"], w["eye"], x1)
    blocks_after(nc, x1, w, out)
    r = _run(nc, [{f"in_{k}": v for k, v in arrays.items()}], core_ids=[0])
    return r.results[0]["out_0"]
```
